# Optimizing a Trainium2 kernel written in Bass

```python
import numpy as np
import jax
import jax.numpy as jnp

def _softmax(x, axis=-1):
    return jax.nn.softmax(x, axis=axis)

def _gelu(x):
    return jax.nn.gelu(x, approximate=True)

def _silu(x):
    return jax.nn.silu(x)

def _sigmoid(x):
    return jax.nn.sigmoid(x)

def _layernorm(x, axis=-1, eps=1e-05):
    m = jnp.mean(x, axis=axis, keepdims=True)
    v = jnp.var(x, axis=axis, keepdims=True)
    return (x - m) / jnp.sqrt(v + eps)

def _scatter_add(tgt, idx, src, axis=0):
    return tgt.at[idx].add(src)

def _segment_sum(src, seg, n):
    return jax.ops.segment_sum(src, seg, n)
kernel_name = 'mk_pixart_seq_d1_seqx_r4_fc7d78'

def setup_inputs(seed: int=0):
    np.random.seed(seed)
    _w = jnp.asarray

    def _rec_inputs():
        import jax
        import jax.numpy as jnp
        _rk = jax.random.key(seed)
        x = -0.0005207 + 1.001 * jax.random.normal(jax.random.fold_in(_rk, 1), (16, 256, 256), jnp.float32)
        _lenS = 256 - jax.random.randint(jax.random.fold_in(_rk, 7), (16,), 0, max(1, 256 // 4) + 1, jnp.int32)
        _lenS2 = 256 - jax.random.randint(jax.random.fold_in(_rk, 8), (16,), 0, max(1, 256 // 4) + 1, jnp.int32)
        cond_1024 = 0.000887014 + 1.03683 * jax.random.normal(jax.random.fold_in(_rk, 11), (16, 256), jnp.float32)
        _ctx_768P = jax.random.normal(jax.random.fold_in(_rk, 12), (16, 16, 192), jnp.float32)
        _ctx_768c = jax.random.dirichlet(jax.random.fold_in(_rk, 512), 0.3 * jnp.ones((16,), jnp.float32), (16, 256))
        _ctx_768t = jnp.einsum('bsk,bkd->bsd', _ctx_768c, _ctx_768P)
        _ctx_768t = _ctx_768t * jax.lax.rsqrt(jnp.mean(jnp.square(_ctx_768t)) + 1e-12) * 0.953939
        ctx_768 = 0.000599585 + 1.00006 * (_ctx_768t + 0.3 * jax.random.normal(jax.random.fold_in(_rk, 612), (16, 256, 192), jnp.float32))
        return (x, cond_1024, ctx_768)
    x, cond_1024, ctx_768 = _rec_inputs()

    def _L0_xcond_setup():
        import jax, jax.numpy as jnp
        import numpy as np
        B, N, M = (2, 256, 128)
        D, H, DH = (256, 16, 64)
        MID = H * DH
        DC = 192
        MULT = 4
        EPS = 1e-05

        def _ln(x, w, b):
            mu = jnp.mean(x, -1, keepdims=True)
            var = jnp.mean((x - mu) ** 2, -1, keepdims=True)
            return (x - mu) * jax.lax.rsqrt(var + EPS) * w + b

        def _sincos(n, d):
            inv = 1.0 / 10000.0 ** (jnp.arange(0, d, 2, dtype=jnp.float32) / d)
            ang = jnp.arange(n, dtype=jnp.float32)[:, None] * inv[None, :]
            return (jnp.sin(ang), jnp.cos(ang))

        def _rope(x, sin, cos):
            s = sin[None, None]
            c = cos[None, None]
            xe = x[..., ::2]
            xo = x[..., 1::2]
            re = xe * c - xo * s
            ro = xe * s + xo * c
            return jnp.stack((re, ro), axis=-1).reshape(x.shape)

        def _heads(t):
            b, n, _ = t.shape
            return t.reshape(b, n, H, DH).transpose(0, 2, 1, 3)

        def _attn(xq, ctx, wq, wkv, wo, bo):
            q = _heads(xq @ wq)
            k, v = jnp.split(ctx @ wkv, 2, axis=-1)
            k = _heads(k)
            v = _heads(v)
            sq, cq = _sincos(q.shape[2], DH)
            sk, ck = _sincos(k.shape[2], DH)
            q = _rope(q, sq, cq)
            k = _rope(k, sk, ck)
            sim = jnp.einsum('bhnd,bhmd->bhnm', q, k) * DH ** (-0.5)
            a = jax.nn.softmax(sim, axis=-1)
            o = jnp.einsum('bhnm,bhmd->bhnd', a, v)
            o = o.transpose(0, 2, 1, 3).reshape(xq.shape[0], xq.shape[1], MID)
            return o @ wo + bo

        def _adaln(x, c, lw, lb, gw, gb, bw, bb):
            g = (c @ gw + gb)[:, None, :]
            bt = (c @ bw + bb)[:, None, :]
            return _ln(x, lw, lb) * (1.0 + g) + bt
        ks = jax.random.split(jax.random.key(seed), 24)
        s = 0.02
        inp = {'x': jax.random.normal(ks[0], (B, N, D), jnp.float32), 'cond': jax.random.normal(ks[1], (B, D), jnp.float32), 'context': jax.random.normal(ks[2], (B, M, DC), jnp.float32), 'ln1_w': jnp.ones((D,), jnp.float32), 'ln1_b': jnp.zeros((D,), jnp.float32), 'g1_w': jax.random.normal(ks[3], (D, D), jnp.float32) * s, 'g1_b': jnp.zeros((D,), jnp.float32), 'b1_w': jax.random.normal(ks[4], (D, D), jnp.float32) * s, 'b1_b': jnp.zeros((D,), jnp.float32), 'ln2_w': jnp.ones((D,), jnp.float32), 'ln2_b': jnp.zeros((D,), jnp.float32), 'g2_w': jax.random.normal(ks[5], (D, D), jnp.float32) * s, 'g2_b': jnp.zeros((D,), jnp.float32), 'b2_w': jax.random.normal(ks[6], (D, D), jnp.float32) * s, 'b2_b': jnp.zeros((D,), jnp.float32), 'sa_wq': jax.random.normal(ks[7], (D, MID), jnp.float32) * s, 'sa_wkv': jax.random.normal(ks[8], (D, 2 * MID), jnp.float32) * s, 'sa_wo': jax.random.normal(ks[9], (MID, D), jnp.float32) * s, 'sa_bo': jnp.zeros((D,), jnp.float32), 'ca_lnc_w': jnp.ones((DC,), jnp.float32), 'ca_lnc_b': jnp.zeros((DC,), jnp.float32), 'ca_wq': jax.random.normal(ks[10], (D, MID), jnp.float32) * s, 'ca_wkv': jax.random.normal(ks[11], (DC, 2 * MID), jnp.float32) * s, 'ca_wo': jax.random.normal(ks[12], (MID, D), jnp.float32) * s, 'ca_bo': jnp.zeros((D,), jnp.float32), 'ff_w1': jax.random.normal(ks[13], (D, MULT * D), jnp.float32) * s, 'ff_b1': jnp.zeros((MULT * D,), jnp.float32), 'ff_w2': jax.random.normal(ks[14], (MULT * D, D), jnp.float32) * s, 'ff_b2': jnp.zeros((D,), jnp.float32)}
        return inp
    _L0_xcond_all = _L0_xcond_setup()
    _L0_xcond_in = {k: v for k, v in _L0_xcond_all.items() if k in ('ln1_w', 'ln1_b', 'g1_w', 'g1_b', 'b1_w', 'b1_b', 'ln2_w', 'ln2_b', 'g2_w', 'g2_b', 'b2_w', 'b2_b', 'sa_wq', 'sa_wkv', 'sa_wo', 'sa_bo', 'ca_lnc_w', 'ca_lnc_b', 'ca_wq', 'ca_wkv', 'ca_wo', 'ca_bo', 'ff_w1', 'ff_b1', 'ff_w2', 'ff_b2')}
    del _L0_xcond_all
    return {'x': x, 'cond_1024': cond_1024, 'ctx_768': ctx_768, 'L0_xcond_ln1_w': _L0_xcond_in['ln1_w'], 'L0_xcond_ln1_b': _L0_xcond_in['ln1_b'], 'L0_xcond_g1_w': _L0_xcond_in['g1_w'], 'L0_xcond_g1_b': _L0_xcond_in['g1_b'], 'L0_xcond_b1_w': _L0_xcond_in['b1_w'], 'L0_xcond_b1_b': _L0_xcond_in['b1_b'], 'L0_xcond_ln2_w': _L0_xcond_in['ln2_w'], 'L0_xcond_ln2_b': _L0_xcond_in['ln2_b'], 'L0_xcond_g2_w': _L0_xcond_in['g2_w'], 'L0_xcond_g2_b': _L0_xcond_in['g2_b'], 'L0_xcond_b2_w': _L0_xcond_in['b2_w'], 'L0_xcond_b2_b': _L0_xcond_in['b2_b'], 'L0_xcond_sa_wq': _L0_xcond_in['sa_wq'], 'L0_xcond_sa_wkv': _L0_xcond_in['sa_wkv'], 'L0_xcond_sa_wo': _L0_xcond_in['sa_wo'], 'L0_xcond_sa_bo': _L0_xcond_in['sa_bo'], 'L0_xcond_ca_lnc_w': _L0_xcond_in['ca_lnc_w'], 'L0_xcond_ca_lnc_b': _L0_xcond_in['ca_lnc_b'], 'L0_xcond_ca_wq': _L0_xcond_in['ca_wq'], 'L0_xcond_ca_wkv': _L0_xcond_in['ca_wkv'], 'L0_xcond_ca_wo': _L0_xcond_in['ca_wo'], 'L0_xcond_ca_bo': _L0_xcond_in['ca_bo'], 'L0_xcond_ff_w1': _L0_xcond_in['ff_w1'], 'L0_xcond_ff_b1': _L0_xcond_in['ff_b1'], 'L0_xcond_ff_w2': _L0_xcond_in['ff_w2'], 'L0_xcond_ff_b2': _L0_xcond_in['ff_b2']}

def reference(x, cond_1024, ctx_768, L0_xcond_ln1_w, L0_xcond_ln1_b, L0_xcond_g1_w, L0_xcond_g1_b, L0_xcond_b1_w, L0_xcond_b1_b, L0_xcond_ln2_w, L0_xcond_ln2_b, L0_xcond_g2_w, L0_xcond_g2_b, L0_xcond_b2_w, L0_xcond_b2_b, L0_xcond_sa_wq, L0_xcond_sa_wkv, L0_xcond_sa_wo, L0_xcond_sa_bo, L0_xcond_ca_lnc_w, L0_xcond_ca_lnc_b, L0_xcond_ca_wq, L0_xcond_ca_wkv, L0_xcond_ca_wo, L0_xcond_ca_bo, L0_xcond_ff_w1, L0_xcond_ff_b1, L0_xcond_ff_w2, L0_xcond_ff_b2):
    import jax
    import jax.numpy as jnp

    def _L0_xcond_ref(x, cond, context, ln1_w, ln1_b, g1_w, g1_b, b1_w, b1_b, ln2_w, ln2_b, g2_w, g2_b, b2_w, b2_b, sa_wq, sa_wkv, sa_wo, sa_bo, ca_lnc_w, ca_lnc_b, ca_wq, ca_wkv, ca_wo, ca_bo, ff_w1, ff_b1, ff_w2, ff_b2):
        import jax, jax.numpy as jnp
        import numpy as np
        B, N, M = (2, 256, 128)
        D, H, DH = (256, 16, 64)
        MID = H * DH
        DC = 192
        MULT = 4
        EPS = 1e-05

        def _ln(x, w, b):
            mu = jnp.mean(x, -1, keepdims=True)
            var = jnp.mean((x - mu) ** 2, -1, keepdims=True)
            return (x - mu) * jax.lax.rsqrt(var + EPS) * w + b

        def _sincos(n, d):
            inv = 1.0 / 10000.0 ** (jnp.arange(0, d, 2, dtype=jnp.float32) / d)
            ang = jnp.arange(n, dtype=jnp.float32)[:, None] * inv[None, :]
            return (jnp.sin(ang), jnp.cos(ang))

        def _rope(x, sin, cos):
            s = sin[None, None]
            c = cos[None, None]
            xe = x[..., ::2]
            xo = x[..., 1::2]
            re = xe * c - xo * s
            ro = xe * s + xo * c
            return jnp.stack((re, ro), axis=-1).reshape(x.shape)

        def _heads(t):
            b, n, _ = t.shape
            return t.reshape(b, n, H, DH).transpose(0, 2, 1, 3)

        def _attn(xq, ctx, wq, wkv, wo, bo):
            q = _heads(xq @ wq)
            k, v = jnp.split(ctx @ wkv, 2, axis=-1)
            k = _heads(k)
            v = _heads(v)
            sq, cq = _sincos(q.shape[2], DH)
            sk, ck = _sincos(k.shape[2], DH)
            q = _rope(q, sq, cq)
            k = _rope(k, sk, ck)
            sim = jnp.einsum('bhnd,bhmd->bhnm', q, k) * DH ** (-0.5)
            a = jax.nn.softmax(sim, axis=-1)
            o = jnp.einsum('bhnm,bhmd->bhnd', a, v)
            o = o.transpose(0, 2, 1, 3).reshape(xq.shape[0], xq.shape[1], MID)
            return o @ wo + bo

        def _adaln(x, c, lw, lb, gw, gb, bw, bb):
            g = (c @ gw + gb)[:, None, :]
            bt = (c @ bw + bb)[:, None, :]
            return _ln(x, lw, lb) * (1.0 + g) + bt
        attn_in = _adaln(x, cond, ln1_w, ln1_b, g1_w, g1_b, b1_w, b1_b)
        x = _attn(attn_in, attn_in, sa_wq, sa_wkv, sa_wo, sa_bo) + x
        cross_in = _adaln(x, cond, ln1_w, ln1_b, g1_w, g1_b, b1_w, b1_b)
        ctx_n = _ln(context, ca_lnc_w, ca_lnc_b)
        x = _attn(cross_in, ctx_n, ca_wq, ca_wkv, ca_wo, ca_bo) + x
        ffn_in = _adaln(x, cond, ln2_w, ln2_b, g2_w, g2_b, b2_w, b2_b)
        h = jax.nn.gelu(ffn_in @ ff_w1 + ff_b1, approximate=False)
        x = h @ ff_w2 + ff_b2 + x
        return x
    x = _L0_xcond_ref(x, cond_1024, ctx_768, L0_xcond_ln1_w, L0_xcond_ln1_b, L0_xcond_g1_w, L0_xcond_g1_b, L0_xcond_b1_w, L0_xcond_b1_b, L0_xcond_ln2_w, L0_xcond_ln2_b, L0_xcond_g2_w, L0_xcond_g2_b, L0_xcond_b2_w, L0_xcond_b2_b, L0_xcond_sa_wq, L0_xcond_sa_wkv, L0_xcond_sa_wo, L0_xcond_sa_bo, L0_xcond_ca_lnc_w, L0_xcond_ca_lnc_b, L0_xcond_ca_wq, L0_xcond_ca_wkv, L0_xcond_ca_wo, L0_xcond_ca_bo, L0_xcond_ff_w1, L0_xcond_ff_b1, L0_xcond_ff_w2, L0_xcond_ff_b2)
    return x

_drawn_inputs = setup_inputs


def setup_inputs(seed=0):
    import zlib

    import numpy as np

    out = dict(_drawn_inputs(seed))
    spreads = {'L0_xcond_ln1_w': (1.0, 0.6),
     'L0_xcond_ln1_b': (0.0, 0.383),
     'L0_xcond_g1_b': (0.0, 0.8),
     'L0_xcond_b1_b': (0.0, 0.359),
     'L0_xcond_ln2_w': (1.0, 0.6),
     'L0_xcond_ln2_b': (0.0, 0.645),
     'L0_xcond_g2_b': (0.0, 0.698),
     'L0_xcond_b2_b': (0.0, 0.764),
     'L0_xcond_sa_bo': (0.0, 0.1),
     'L0_xcond_ca_lnc_w': (1.0, 0.6),
     'L0_xcond_ca_lnc_b': (0.0, 0.532),
     'L0_xcond_ca_bo': (0.0, 0.1),
     'L0_xcond_ff_b1': (0.0, 0.1),
     'L0_xcond_ff_b2': (0.0, 0.1)}
    factors = {'L0_xcond_g1_w': 7.249, 'L0_xcond_sa_wq': 8.0, 'L0_xcond_ca_wq': 8.0}
    for name, (base, spread) in spreads.items():
        noise = np.random.default_rng([zlib.crc32(name.encode()), seed]).standard_normal(out[name].shape)
        drawn = base * np.exp(spread * noise) if base else spread * noise
        out[name] = jnp.asarray(drawn.astype(out[name].dtype))
    for name, factor in factors.items():
        out[name] = (out[name] * factor).astype(out[name].dtype)
    return out
```

```python
from contextlib import ExitStack

import concourse.bass as bass
from concourse import mybir

F32 = mybir.dt.float32
ALU = mybir.AluOpType
ACT = mybir.ActivationFunctionType
AX = mybir.AxisListType

P = 128
BATCH, N, D = 16, 256, 256
H, DH = 16, 64
MID = H * DH
DC = 192
FF = 4 * D
EPS = 1e-5
TT = N // P
KT = D // P
CHUNK = 512
HALVES = MID // CHUNK
CH_HEADS = CHUNK // DH
PAIRS = H // 2
MT = MID // P
SLOTS = 2
ITERS = BATCH // SLOTS
LAST_STEP = H + 4

PASSES = [("self", 0), ("self", 1), ("cross", 0), ("cross", 1)]


def projection_units(n):
    chunks = [("chunk", n, x, tt, half) for tt in range(TT) for x in "qkv" for half in range(HALVES)]
    units, late = [], []
    for i, c in enumerate(chunks):
        units.append(c)
        if c[2] != "v":
            late.append((i + 3, ("turn",) + c[1:]))
        while late and late[0][0] <= i:
            units.append(late.pop(0)[1])
    return units + [t for _, t in late]


def make_schedule():
    s = [("stats", ("ln", 0)), ("norm", ("ln", 0)), ("bank", ("lnT", ("ln", 0)))]
    s += [("bank", u) for u in projection_units(0)]
    for n in range(len(PASSES)):
        after = [[] for _ in range(LAST_STEP)]
        if n:
            after[0].append(("bank", ("wo", n - 1)))
        following = ("ln", n + 1) if n < 3 else ("ff", 0)
        after[0].append(("stats", following))
        after[1].append(("norm", following))
        after[2].append(("bank", ("lnT", following)))
        if n < 3:
            if PASSES[n + 1][0] == "cross":
                after[1].append(("stats", ("ctx", n + 1)))
                after[2].append(("norm", ("ctx", n + 1)))
                after[3].append(("bank", ("lnT", ("ctx", n + 1))))
            units = projection_units(n + 1)
            for i, u in enumerate(units):
                after[3 + (i * (LAST_STEP - 4)) // len(units)].append(("bank", u))
        for step in range(LAST_STEP):
            s.append(("step", (n, step)))
            s += after[step]
    s += [("bank", ("hidden", 0, j)) for j in range(FF // P // 2)]
    s += [("bank", ("wo", 3)), ("stats", ("ff", 1)), ("bank", ("out", 0)), ("store", 0), ("norm", ("ff", 1)),
          ("bank", ("lnT", ("ff", 1)))]
    s += [("bank", ("hidden", 1, j)) for j in range(FF // P // 2)]
    s += [("bank", ("out", 1)), ("store", 1)]
    return s


SCHEDULE = make_schedule()
BANK_USES = [x for kind, x in SCHEDULE if kind == "bank"]
NORMS = [x for kind, x in SCHEDULE if kind == "stats"]
RESIDUALS = [x for x in BANK_USES if x[0] in ("wo", "out")]
TURNS = [x for x in BANK_USES if x[0] == "turn"]
V_CHUNKS = [x for x in BANK_USES if x[0] == "chunk" and x[2] == "v"]
assert len(BANK_USES) % 2 == 0

BIAS_AT = {("step", (0, 2)): [0], ("step", (0, 6)): [1], ("step", (2, 2)): [2], ("step", (3, 2)): [3],
           ("step", (3, 8)): [4], ("bank", ("wo", 3)): [5]}
VECTOR_LOADS = 3 + 10 * KT + 1


def vector_loads(t, bias_row, vec, ff_b1):
    for x, name in (("self", "sa_bo"), ("cross", "ca_bo"), ("ff", "ff_b2")):
        yield bias_row[x][:], t[f"L0_xcond_{name}"].unsqueeze(0).broadcast_to([P, D])
    for x, dst in vec.items():
        src = t[f"L0_xcond_{x}"].unsqueeze(1)
        for k, (col, rows) in enumerate([(0, P), (P, DC - P if x.startswith("ca") else P)]):
            yield dst[0:rows, k:k + 1], src[col:col + rows, :]
    yield ff_b1[:], t["L0_xcond_ff_b1"].rearrange("(t p) -> p t", p=P)


def block_kernel(nc, t):
    with ExitStack() as ctx:
        def sb(name, shape, dt=F32):
            return ctx.enter_context(nc.sbuf_tensor(name, shape, dt))

        def pb(name):
            return ctx.enter_context(nc.psum_tensor(name, [P, 512], F32))

        def sem(name):
            return ctx.enter_context(nc.semaphore(name))

        w_q = {"self": sb("w_sa_q", [P, KT, MID]), "cross": sb("w_ca_q", [P, KT, MID])}
        w_kv = {"self": sb("w_sa_kv", [P, KT, 2 * MID]), "cross": sb("w_ca_kv", [P, KT, 2 * MID])}
        w_o = {"self": sb("w_sa_o", [P, MT, D]), "cross": sb("w_ca_o", [P, MT, D])}
        w_1 = sb("w_1", [P, KT, FF])
        w_2 = sb("w_2", [P, FF // P, D])
        bias_row = {x: sb(f"bias_{x}", [P, D]) for x in ("self", "cross", "ff")}
        vec = {x: sb(f"vec_{x}", [P, KT]) for x in (
            "ln1_w", "ln1_b", "g1_b", "b1_b", "ln2_w", "ln2_b", "g2_b", "b2_b", "ca_lnc_w", "ca_lnc_b")}
        ff_b1 = sb("ff_b1", [P, FF // P])
        rope_cos = {x: sb(f"rope_cos_{x}", [P, TT, DH]) for x in "qk"}
        rope_sin = {x: sb(f"rope_sin_{x}", [P, TT, DH]) for x in "qk"}
        ident = sb("ident", [P, P])
        minus_half = sb("minus_half", [P, TT])
        cond = sb("cond", [BATCH, D])
        cond_T = sb("cond_T", [P, KT, BATCH])
        gain = {x: sb(f"gain_{x}", [P, KT, BATCH]) for x in ("1", "2")}
        shift = {x: sb(f"shift_{x}", [P, KT, BATCH]) for x in ("1", "2")}
        one_plus_g = sb("one_plus_g", [P, 2, KT, BATCH])

        x_in = [sb(f"x_in{s}", [P, TT, D]) for s in range(SLOTS)]
        c_in = [sb(f"c_in{s}", [P, TT, DC]) for s in range(SLOTS)]
        x_mid = {(k, s): sb(f"x_mid_{k}{s}", [P, TT, D]) for k in ("self", "cross") for s in range(SLOTS)}
        x_out = [sb(f"x_out{s}", [P, TT, D]) for s in range(SLOTS)]
        biased = [sb(f"biased{r}", [P, TT, D]) for r in range(len(RESIDUALS))]
        stats = [sb(f"stats{i}", [P, TT, 6]) for i in range(2)]
        moments = [sb(f"moments{i}", [P, TT, 2]) for i in range(2)]
        var_eps = [sb(f"var_eps{i}", [P, TT]) for i in range(2)]
        rstd = [sb(f"rstd{i}", [P, TT]) for i in range(2)]
        x_hat = [sb(f"x_hat{i}", [P, TT, D]) for i in range(2)]
        a_T = sb("a_T", [P, KT, N])
        c_T = sb("c_T", [P, KT, N])
        x_cos = [sb(f"x_cos{i}", [P, CHUNK]) for i in range(2)]
        x_sin = [sb(f"x_sin{i}", [P, CHUNK]) for i in range(2)]
        roped = [sb(f"roped{i}", [P, CHUNK]) for i in range(2)]
        q_T = [sb(f"q_T{i}", [P, PAIRS, N]) for i in range(2)]
        k_T = [sb(f"k_T{i}", [P, PAIRS, N]) for i in range(2)]
        w_cond = {x: k_T[1][:].rearrange("p a n -> p (a n)")[:, i * KT * D:(i + 1) * KT * D].rearrange(
            "p (t n) -> p t n", t=KT) for i, x in enumerate(("g1", "b1", "g2", "b2"))}
        v = [sb(f"v{i}", [P, TT, MID]) for i in range(2)]
        o_T = sb("o_T", [P, PAIRS, N])
        h_T = q_T[0]
        NP = 4
        probs = [sb(f"probs{i}", [P, TT, N]) for i in range(NP)]
        probs_T = [sb(f"probs_T{i}", [P, TT, N]) for i in range(2)]
        neg_max = sb("neg_max", [P, NP, TT])
        row_sum = sb("row_sum", [P, NP, TT])
        row_inv = sb("row_inv", [P, NP, TT])

        bank = [pb("bank0"), pb("bank1")]
        ps_scores = [pb("ps_scores0"), pb("ps_scores1")]
        ps_probs_T = [pb("ps_probs_T0"), pb("ps_probs_T1")]
        ps_o = [pb("ps_o0"), pb("ps_o1")]

        w_loaded = {x: sem(f"loaded_{x}") for x in (
            "vectors", "rope", "cond", "sa_wq", "sa_wkv", "sa_wo", "ca_wq", "ca_wkv", "ca_wo", "ff_w1", "ff_w2")}
        x_loaded = [sem(f"x_loaded{s}") for s in range(SLOTS)]
        c_loaded = [sem(f"c_loaded{s}") for s in range(SLOTS)]
        stored = [sem(f"stored{s}") for s in range(SLOTS)]
        ident_made = sem("ident_made")
        cond_turned, cond_copied, cond_projected, cond_ready = (
            sem("cond_turned"), sem("cond_copied"), sem("cond_projected"), sem("cond_ready"))
        bank_filled = sem("bank_filled")
        stats_made, moments_made, var_made, rstd_made, x_hat_made = (
            sem("stats_made"), sem("moments_made"), sem("var_made"), sem("rstd_made"), sem("x_hat_made"))
        a_T_ready = sem("a_T_ready")
        biased_made, residual_made = sem("biased_made"), sem("residual_made")
        parts_made, roped_made = sem("parts_made"), sem("roped_made")
        qk_T_ready, v_ready = sem("qk_T_ready"), sem("v_ready")
        scores_made, max_made, probs_made, inv_made, probs_scaled = (
            sem("scores_made"), sem("max_made"), sem("probs_made"), sem("inv_made"), sem("probs_scaled"))
        probs_turned, probs_T_ready, pv_made, o_T_ready = (
            sem("probs_turned"), sem("probs_T_ready"), sem("pv_made"), sem("o_T_ready"))
        hidden_ready = sem("hidden_ready")
        sp_passed, dve_passed = sem("sp_passed"), sem("dve_passed")

        CREDIT = 32
        credited = [*x_loaded, *c_loaded, *stored, bank_filled, stats_made, moments_made, var_made, rstd_made,
                    x_hat_made, a_T_ready, biased_made, residual_made, parts_made, roped_made,
                    qk_T_ready, v_ready, scores_made, max_made, probs_made, inv_made, probs_scaled,
                    probs_turned, probs_T_ready, pv_made, o_T_ready, hidden_ready]

        def nth(it, per_iteration, ordinal):
            return it * per_iteration + (ordinal + 1 + CREDIT)

        def nth_dma(it):
            return it * 16 + (16 + CREDIT)

        def chunk_no(u):
            _, n, x, tt, half = u
            return ((n * TT + tt) * 2 + "qk".index(x)) * HALVES + half

        TURNS_BY_CHUNK = sorted(TURNS, key=chunk_no)
        QK_CHUNKS = len(PASSES) * TT * 2 * HALVES
        HEADS = len(PASSES) * H
        QUADS = HEADS // 4

        def bank_of(w):
            return bank[w % 2]

        def turned(it, things, i):
            if i < 0:
                it, i = it - 1, i + len(things)
            return nth(it, len(BANK_USES), BANK_USES.index(things[i]))

        def emptied(it, w):
            if w < 0:
                it, w = it - 1, w + len(BANK_USES)
            u = BANK_USES[w]
            if u[0] == "lnT":
                return a_T_ready, nth(it, len(NORMS), NORMS.index(u[1]))
            if u[0] == "turn":
                return qk_T_ready, nth(it, QK_CHUNKS, TURNS.index(u))
            if u[0] == "hidden":
                return hidden_ready, nth(it, FF // P, u[1] * (FF // P // 2) + u[2])
            if u[0] in ("wo", "out"):
                return residual_made, nth(it, len(RESIDUALS), RESIDUALS.index(u))
            if u[2] == "v":
                return v_ready, nth(it, QK_CHUNKS // 2, V_CHUNKS.index(u))
            return parts_made, nth(it, QK_CHUNKS, chunk_no(u))

        def source(x):
            kind, n = x
            if kind == "ctx":
                return c_in[PASSES[n][1]]
            if kind == "ff":
                return x_mid["cross", n]
            return x_in[n] if n < 2 else x_mid["self", n - 2]

        def residual_source(r):
            kind, n = r
            if kind == "out":
                return x_mid["cross", n]
            return x_in[n] if n < 2 else x_mid["self", n - 2]

        def residual_target(r):
            kind, n = r
            return x_out[n] if kind == "out" else x_mid[PASSES[n][0], PASSES[n][1]]

        def widths(kind):
            return [(0, P), (P, DC - P)] if kind == "ctx" else [(0, P), (P, P)]

        block = ctx.enter_context(nc.Block())

        @block.sync
        def _(sp):
            def load(dst, src, s):
                sp.dma_start(dst, src).then_inc(s, 16)

            def load_x(b, s):
                sp.dma_start(x_in[s][:], t["x"][bass.ds(b, 1), :, :].rearrange(
                    "b (t p) d -> p (b t) d", p=P)).then_inc(x_loaded[s], 16)

            def load_c(b, s):
                sp.dma_start(c_in[s][:], t["ctx_768"][bass.ds(b, 1), :, :].rearrange(
                    "b (t p) d -> p (b t) d", p=P)).then_inc(c_loaded[s], 16)

            load_x(0, 0)
            load(cond[:], t["cond_1024"], w_loaded["cond"])
            for x in ("g1", "b1"):
                load(w_cond[x], t[f"L0_xcond_{x}_w"].rearrange("(t p) n -> p t n", p=P), w_loaded["cond"])
            load(w_q["self"][:], t["L0_xcond_sa_wq"].rearrange("(t p) n -> p t n", p=P), w_loaded["sa_wq"])
            load(w_kv["self"][:], t["L0_xcond_sa_wkv"].rearrange("(t p) n -> p t n", p=P), w_loaded["sa_wkv"])
            load_x(1, 1)
            load_c(0, 0)
            load_c(1, 1)
            load(w_o["self"][:], t["L0_xcond_sa_wo"].rearrange("(t p) n -> p t n", p=P), w_loaded["sa_wo"])
            load(w_q["cross"][:], t["L0_xcond_ca_wq"].rearrange("(t p) n -> p t n", p=P), w_loaded["ca_wq"])
            load(w_kv["cross"][:, 0, :], t["L0_xcond_ca_wkv"][0:P, :], w_loaded["ca_wkv"])
            load(w_kv["cross"][0:DC - P, 1, :], t["L0_xcond_ca_wkv"][P:DC, :], w_loaded["ca_wkv"])
            load(w_o["cross"][:], t["L0_xcond_ca_wo"].rearrange("(t p) n -> p t n", p=P), w_loaded["ca_wo"])
            load(w_1[:], t["L0_xcond_ff_w1"].rearrange("(t p) n -> p t n", p=P), w_loaded["ff_w1"])
            load(w_2[:], t["L0_xcond_ff_w2"].rearrange("(t p) n -> p t n", p=P), w_loaded["ff_w2"])
            with sp.Fori(1, ITERS) as it:
                for s in range(SLOTS):
                    sp.wait_ge(x_hat_made, nth(it - 1, len(NORMS), NORMS.index(("ln", s))))
                    sp.sem_inc(sp_passed, 1)
                    sp.wait_ge(biased_made, nth(it - 1, len(RESIDUALS), s))
                    sp.sem_inc(sp_passed, 1)
                    load_x(it * SLOTS + s, s)
                for s in range(SLOTS):
                    sp.wait_ge(x_hat_made, nth(it - 1, len(NORMS), NORMS.index(("ctx", 2 + s))))
                    sp.sem_inc(sp_passed, 1)
                    load_c(it * SLOTS + s, s)

        @block.gpsimd
        def _(pool):
            for s in credited:
                pool.sem_inc(s, CREDIT)
            nc.gpsimd.memset(minus_half[:], -0.5)
            nc.gpsimd.memset(ident[:], 0.0).then_inc(ident_made, 1)
            pool.wait_ge(ident_made, 1)
            nc.gpsimd.affine_select(out=ident[:], in_=ident[:], compare_op=ALU.not_equal, fill=1.0, base=0,
                                    pattern=[[-1, P]], channel_multiplier=1).then_inc(ident_made, 1)
            pool.wait_ge(w_loaded["vectors"], 16 * VECTOR_LOADS)

            def add_bias(it, r):
                kind, n = RESIDUALS[r]
                if kind == "wo" and n < 2:
                    pool.wait_ge(x_loaded[n], nth_dma(it))
                    pool.wait_ge(residual_made, nth(it, len(RESIDUALS), r - len(RESIDUALS)))
                else:
                    src = RESIDUALS.index(("wo", n - 2) if kind == "wo" else ("wo", n + 2))
                    pool.wait_ge(residual_made, nth(it, len(RESIDUALS), src))
                row = bias_row["ff" if kind == "out" else PASSES[n][0]]
                nc.gpsimd.tensor_tensor(out=biased[r][:], in0=residual_source(RESIDUALS[r])[:],
                                        in1=row[:].unsqueeze(1).broadcast_to([P, TT, D]),
                                        op=ALU.add).then_inc(biased_made, 1)

            with pool.Fori(0, ITERS) as it:
                for kind, x in SCHEDULE:
                    if kind == "stats":
                        n = NORMS.index(x)
                        pool.wait_ge(var_made, nth(it, len(NORMS), n))
                        nc.gpsimd.tensor_tensor(out=rstd[n % 2][:], in0=var_eps[n % 2][:], in1=minus_half[:],
                                                op=ALU.pow).then_inc(rstd_made, 1)
                    elif kind == "bank" and x[0] == "chunk" and x[2] != "v":
                        c = chunk_no(x)
                        pool.wait_ge(parts_made, nth(it, QK_CHUNKS, c))
                        pool.wait_ge(bank_filled, turned(it, TURNS_BY_CHUNK, c - 2))
                        nc.gpsimd.tensor_tensor(out=roped[c % 2][:], in0=x_cos[c % 2][:], in1=x_sin[c % 2][:],
                                                op=ALU.add).then_inc(roped_made, 1)
                    elif kind == "step":
                        n, step = x
                        if 1 <= step <= H:
                            h = n * H + step - 1
                            pool.wait_ge(inv_made, nth(it, HEADS, h))
                            nc.gpsimd.tensor_tensor(
                                out=probs[h % NP][:], in0=probs[h % NP][:],
                                in1=row_inv[:, h % NP, :].unsqueeze(2).broadcast_to([P, TT, N]),
                                op=ALU.mult).then_inc(probs_scaled, 1)
                    if (kind, x) in BIAS_AT:
                        for r in BIAS_AT[kind, x]:
                            add_bias(it, r)

        @block.vector
        def _(dve):
            dve.wait_ge(cond_turned, 1)
            nc.vector.tensor_copy(cond_T[:], bank[0][:, 0:KT * BATCH].rearrange(
                "p (t b) -> p t b", t=KT)).then_inc(cond_copied, 1)
            dve.wait_ge(w_loaded["vectors"], 16 * VECTOR_LOADS)
            dve.wait_ge(cond_projected, 1)
            made = bank[1][:, 0:4 * KT * BATCH].rearrange("p (m t b) -> p m t b", m=4, t=KT)
            for i, x in enumerate("12"):
                for k in range(KT):
                    nc.vector.tensor_scalar(one_plus_g[:, i, k, :], made[:, 2 * i, k, :], vec[f"g{x}_b"][:, k:k + 1],
                                            1.0, ALU.add, ALU.add)
                    last = nc.vector.tensor_scalar(shift[x][:, k, :], made[:, 2 * i + 1, k, :],
                                                   vec[f"b{x}_b"][:, k:k + 1], None, ALU.add)
            last.then_inc(cond_ready, 1)
            dve.wait_ge(cond_ready, 1)
            for i, x in enumerate("12"):
                for k in range(KT):
                    nc.vector.tensor_scalar(gain[x][:, k, :], one_plus_g[:, i, k, :], vec[f"ln{x}_w"][:, k:k + 1],
                                            None, ALU.mult)
                    last = nc.vector.scalar_tensor_tensor(
                        out=shift[x][:, k, :], in0=one_plus_g[:, i, k, :], scalar=vec[f"ln{x}_b"][:, k:k + 1],
                        in1=shift[x][:, k, :], op0=ALU.mult, op1=ALU.add)
            last.then_inc(cond_ready, 1)
            dve.wait_ge(cond_ready, 2)
            dve.wait_ge(w_loaded["rope"], 16 * 4)

            def layernorm_stats(it, n):
                kind, at = NORMS[n]
                src, j = source(NORMS[n]), n % 2
                if kind == "ctx":
                    dve.wait_ge(c_loaded[PASSES[at][1]], nth_dma(it))
                elif kind == "ln" and at < 2:
                    dve.wait_ge(x_loaded[at], nth_dma(it))
                else:
                    r = RESIDUALS.index(("wo", at - 2 if kind == "ln" else at + 2))
                    dve.wait_ge(residual_made, nth(it, len(RESIDUALS), r))
                dve.wait_ge(x_hat_made, nth(it, len(NORMS), n - 2))
                for tt in range(TT):
                    last = nc.vector.bn_stats(out=stats[j][:, tt, :], in_=src[:, tt, :])
                last.then_inc(stats_made, 1)
                dve.wait_ge(stats_made, nth(it, len(NORMS), n))
                dve.sem_inc(dve_passed, 1)
                for tt in range(TT):
                    last = nc.vector.bn_aggr(out=moments[j][:, tt, :], in_=stats[j][:, tt, :])
                last.then_inc(moments_made, 1)
                dve.wait_ge(moments_made, nth(it, len(NORMS), n))
                nc.vector.tensor_scalar(var_eps[j][:], moments[j][:, :, 1], EPS, None, ALU.add).then_inc(var_made, 1)

            def layernorm_apply(it, n):
                src, j = source(NORMS[n]), n % 2
                width = DC if NORMS[n][0] == "ctx" else D
                dve.wait_ge(rstd_made, nth(it, len(NORMS), n))
                dve.wait_ge(bank_filled, turned(it, [("lnT", x) for x in NORMS], n - 2))
                for tt in range(TT):
                    last = nc.vector.tensor_scalar(x_hat[j][:, tt, 0:width], src[:, tt, :], moments[j][:, tt, 0:1],
                                                   rstd[j][:, tt:tt + 1], ALU.subtract, ALU.mult)
                last.then_inc(x_hat_made, 1)

            def empty_bank(it, w):
                u = BANK_USES[w]
                src = bank_of(w)
                if u[0] == "lnT":
                    kind, at = u[1]
                    dve.wait_ge(bank_filled, nth(it, len(BANK_USES), w))
                    dst = c_T if kind == "ctx" else a_T
                    for k, (_, rows) in enumerate(widths(kind)):
                        if kind == "ctx":
                            g, b = vec["ca_lnc_w"][0:rows, k:k + 1], vec["ca_lnc_b"][0:rows, k:k + 1]
                        else:
                            which = "2" if kind == "ff" else "1"
                            s = at if kind == "ff" else PASSES[at][1]
                            g = gain[which][:, k, bass.ds(it * SLOTS + s, 1)]
                            b = shift[which][:, k, bass.ds(it * SLOTS + s, 1)]
                        last = nc.vector.tensor_scalar(dst[0:rows, k, :], src[0:rows, k * N:(k + 1) * N], g, b,
                                                       ALU.mult, ALU.add)
                    last.then_inc(a_T_ready, 1)
                elif u[0] == "chunk" and u[2] != "v":
                    _, n, x, tt, half = u
                    c = chunk_no(u)
                    dve.wait_ge(bank_filled, nth(it, len(BANK_USES), w))
                    dve.wait_ge(roped_made, nth(it, QK_CHUNKS, c - 2))
                    heads = "p (h d) -> p h d"
                    cos = rope_cos[x][:, tt, :].unsqueeze(1).broadcast_to([P, CH_HEADS, DH])
                    nc.vector.tensor_tensor(out=x_cos[c % 2][:].rearrange(heads, d=DH),
                                            in0=src[:].rearrange(heads, d=DH), in1=cos, op=ALU.mult)
                    pairs = "p (h j two) -> p h j two"
                    sin = rope_sin[x][:, tt, :].rearrange("p (j two) -> p j two", two=2)
                    sin = sin.unsqueeze(1).broadcast_to([P, CH_HEADS, DH // 2, 2])
                    nc.vector.tensor_tensor(out=x_sin[c % 2][:].rearrange(pairs, two=2, j=DH // 2),
                                            in0=src[:].rearrange(pairs, two=2, j=DH // 2)[:, :, :, ::-1],
                                            in1=sin, op=ALU.mult).then_inc(parts_made, 1)
                elif u[0] in ("wo", "out"):
                    r = RESIDUALS.index(u)
                    dve.wait_ge(bank_filled, nth(it, len(BANK_USES), w))
                    dve.wait_ge(biased_made, nth(it, len(RESIDUALS), r))
                    if u[0] == "out":
                        dve.wait_ge(stored[u[1]], nth_dma(it - 1))
                    nc.vector.tensor_tensor(out=residual_target(u)[:], in0=src[:].rearrange("p (t d) -> p t d", t=TT),
                                            in1=biased[r][:], op=ALU.add).then_inc(residual_made, 1)

            with dve.Fori(0, ITERS) as it:
                for kind, x in SCHEDULE:
                    if kind == "stats":
                        layernorm_stats(it, NORMS.index(x))
                    elif kind == "norm":
                        layernorm_apply(it, NORMS.index(x))
                    elif kind == "bank":
                        empty_bank(it, BANK_USES.index(x))
                    elif kind == "step":
                        n, step = x
                        if step < H:
                            h = n * H + step
                            dve.wait_ge(scores_made, nth(it, HEADS, h))
                            nc.vector.tensor_reduce(
                                out=neg_max[:, h % NP, :], in_=ps_scores[h % 2][:].rearrange("p (t m) -> p t m", t=TT),
                                axis=AX.X, op=ALU.max, negate=True).then_inc(max_made, 1)
                        if 1 <= step <= H:
                            h = n * H + step - 1
                            dve.wait_ge(probs_made, nth(it, HEADS, h))
                            nc.vector.reciprocal(row_inv[:, h % NP, :], row_sum[:, h % NP, :]).then_inc(inv_made, 1)
                        if 3 <= step < H + 3:
                            h = n * H + step - 3
                            dve.wait_ge(probs_turned, nth(it, HEADS, h))
                            dve.wait_ge(pv_made, nth(it, HEADS, h - 2))
                            nc.vector.tensor_copy(probs_T[h % 2][:].rearrange("p t n -> p (t n)"),
                                                  ps_probs_T[h % 2][:]).then_inc(probs_T_ready, 1)

        @block.scalar
        def _(act):
            for dst, src in vector_loads(t, bias_row, vec, ff_b1):
                act.dma_start(dst, src, allow_slow_non_contiguous=True).then_inc(w_loaded["vectors"], 16)
            for x in "qk":
                act.dma_start(rope_cos[x][:], t[f"rope_cos_{x}"].rearrange("(t p) d -> p t d", p=P)).then_inc(w_loaded["rope"], 16)
                act.dma_start(rope_sin[x][:], t[f"rope_sin_{x}"].rearrange("(t p) d -> p t d", p=P)).then_inc(w_loaded["rope"], 16)
            for x in ("g2", "b2"):
                act.dma_start(w_cond[x], t[f"L0_xcond_{x}_w"].rearrange("(t p) n -> p t n", p=P)).then_inc(w_loaded["cond"], 16)

            def empty_bank(it, w):
                u = BANK_USES[w]
                src = bank_of(w)
                if u[0] == "turn":
                    _, n, x, tt, half = u
                    act.wait_ge(bank_filled, nth(it, len(BANK_USES), w))
                    dst = (q_T if x == "q" else k_T)[n % 2]
                    per = CH_HEADS // 2
                    nc.scalar.activation(dst[:, half * per:(half + 1) * per, tt * P:(tt + 1) * P],
                                         src[:].rearrange("p (a n) -> p a n", a=per), ACT.Copy).then_inc(qk_T_ready, 1)
                elif u[0] == "chunk" and u[2] == "v":
                    _, n, x, tt, half = u
                    act.wait_ge(bank_filled, nth(it, len(BANK_USES), w))
                    nc.scalar.activation(v[n % 2][:, tt, half * CHUNK:(half + 1) * CHUNK], src[:],
                                         ACT.Copy).then_inc(v_ready, 1)
                elif u[0] == "hidden":
                    _, s, j = u
                    act.wait_ge(bank_filled, nth(it, len(BANK_USES), w))
                    for i in range(2):
                        last = nc.scalar.activation(h_T[:, 2 * j + i, :], src[:, i * N:(i + 1) * N], ACT.Gelu,
                                                    bias=ff_b1[:, 2 * j + i:2 * j + i + 1])
                    last.then_inc(hidden_ready, 1)

            act.wait_ge(w_loaded["vectors"], 16 * VECTOR_LOADS)
            with act.Fori(0, ITERS) as it:
                for kind, x in SCHEDULE:
                    if kind == "bank":
                        empty_bank(it, BANK_USES.index(x))
                    elif kind == "store":
                        act.wait_ge(residual_made, nth(it, len(RESIDUALS), RESIDUALS.index(("out", x))))
                        act.dma_start(t["out"][bass.ds(it * SLOTS + x, 1), :, :].rearrange("b (t p) d -> p (b t) d", p=P),
                                      x_out[x][:]).then_inc(stored[x], 16)
                    elif kind == "step":
                        n, step = x
                        if step < H:
                            h = n * H + step
                            act.wait_ge(max_made, nth(it, HEADS, h))
                            act.wait_ge(probs_turned, nth(it, HEADS, h - NP))
                            for tt in range(TT):
                                last = nc.scalar.activation(probs[h % NP][:, tt, :], ps_scores[h % 2][:, tt * N:(tt + 1) * N],
                                                            ACT.Exp, bias=neg_max[:, h % NP, tt:tt + 1],
                                                            accum_out=row_sum[:, h % NP, tt:tt + 1])
                            last.then_inc(probs_made, 1)
                        done = step - 5
                        if done >= 0 and done % 4 == 3 or step == LAST_STEP - 1:
                            quad = n * 4 + (done // 4 if step < LAST_STEP - 1 else 3)
                            act.wait_ge(pv_made, nth(it, HEADS, 4 * quad + 3))
                            q = quad % 4
                            nc.scalar.activation(o_T[:, 2 * q:2 * q + 2, :].rearrange("p a n -> p (a n)"),
                                                 ps_o[quad % 2][:], ACT.Copy).then_inc(o_T_ready, 1)
            for s in range(SLOTS):
                act.wait_ge(stored[s], CREDIT + 16 * ITERS)

        @block.tensor
        def _(pe):
            pe.wait_ge(ident_made, 2)
            pe.wait_ge(w_loaded["cond"], 16 * 5)
            for k in range(KT):
                last = nc.tensor.transpose(bank[0][:, k * BATCH:(k + 1) * BATCH], cond[:, k * P:(k + 1) * P],
                                           ident[0:BATCH, 0:BATCH])
            last.then_inc(cond_turned, 1)
            pe.wait_ge(cond_copied, 1)
            for m, x in enumerate(("g1", "b1", "g2", "b2")):
                for dt in range(KT):
                    col = (m * KT + dt) * BATCH
                    for k in range(KT):
                        last = nc.tensor.matmul(bank[1][:, col:col + BATCH], w_cond[x][:, k, dt * P:(dt + 1) * P],
                                                cond_T[:, k, :], start=(k == 0), stop=(k == KT - 1))
            last.then_inc(cond_projected, 1)
            pe.wait_ge(cond_ready, 1)

            def fill_bank(it, w):
                u = BANK_USES[w]
                dst = bank_of(w)
                pe.wait_ge(*emptied(it, w - 2))
                if u[0] == "lnT":
                    i = NORMS.index(u[1])
                    pe.wait_ge(x_hat_made, nth(it, len(NORMS), i))
                    for k, (col, rows) in enumerate(widths(u[1][0])):
                        for tt in range(TT):
                            last = nc.tensor.transpose(dst[0:rows, k * N + tt * P:k * N + (tt + 1) * P],
                                                       x_hat[i % 2][:, tt, col:col + rows], ident[:])
                elif u[0] == "chunk":
                    _, n, x, tt, half = u
                    kind = PASSES[n][0]
                    side = "ctx" if kind == "cross" and x != "q" else "ln"
                    weights = w_q[kind] if x == "q" else w_kv[kind]
                    col = half * CHUNK + (MID if x == "v" else 0)
                    if (x, tt, half) in (("q", 0, 0), ("k", 0, 0)):
                        pe.wait_ge(w_loaded[f"{'sa' if kind == 'self' else 'ca'}_w{'q' if x == 'q' else 'kv'}"],
                                   32 if side == "ctx" else 16)
                        pe.wait_ge(a_T_ready, nth(it, len(NORMS), NORMS.index((side, n))))
                    for k, (_, rows) in enumerate(widths(side)):
                        last = nc.tensor.matmul(dst[:], (c_T if side == "ctx" else a_T)[0:rows, k, tt * P:(tt + 1) * P],
                                                weights[0:rows, k, col:col + CHUNK], start=(k == 0), stop=(k == KT - 1))
                elif u[0] == "turn":
                    c = chunk_no(u)
                    pe.wait_ge(roped_made, nth(it, QK_CHUNKS, c))
                    for a in range(CH_HEADS // 2):
                        last = nc.tensor.transpose(dst[:, a * P:(a + 1) * P], roped[c % 2][:, a * P:(a + 1) * P], ident[:])
                elif u[0] == "wo":
                    n = u[1]
                    kind = PASSES[n][0]
                    pe.wait_ge(w_loaded["sa_wo" if kind == "self" else "ca_wo"], 16)
                    pe.wait_ge(o_T_ready, nth(it, QUADS, 4 * n + 3))
                    for tt in range(TT):
                        for m in range(MT):
                            last = nc.tensor.matmul(dst[:, tt * D:(tt + 1) * D], o_T[:, m, tt * P:(tt + 1) * P],
                                                    w_o[kind][:, m, :], start=(m == 0), stop=(m == MT - 1))
                elif u[0] == "hidden":
                    _, s, j = u
                    if j == 0:
                        pe.wait_ge(w_loaded["ff_w1"], 16)
                        pe.wait_ge(a_T_ready, nth(it, len(NORMS), NORMS.index(("ff", s))))
                    for i in range(2):
                        for k in range(KT):
                            last = nc.tensor.matmul(dst[:, i * N:(i + 1) * N], w_1[:, k, (2 * j + i) * P:(2 * j + i + 1) * P],
                                                    a_T[:, k, :], start=(k == 0), stop=(k == KT - 1))
                else:
                    s = u[1]
                    pe.wait_ge(w_loaded["ff_w2"], 16)
                    pe.wait_ge(hidden_ready, nth(it, FF // P, (s + 1) * (FF // P // 2) - 1))
                    for tt in range(TT):
                        for m in range(FF // P):
                            last = nc.tensor.matmul(dst[:, tt * D:(tt + 1) * D], h_T[:, m, tt * P:(tt + 1) * P],
                                                    w_2[:, m, :], start=(m == 0), stop=(m == FF // P - 1))
                return last

            with pe.Fori(0, ITERS) as it:
                for kind, x in SCHEDULE:
                    if kind == "bank":
                        fill_bank(it, BANK_USES.index(x)).then_inc(bank_filled, 1)
                    elif kind == "step":
                        n, step = x
                        if step < H:
                            h = n * H + step
                            if step == 0:
                                pe.wait_ge(qk_T_ready, nth(it, QK_CHUNKS, (n + 1) * (QK_CHUNKS // 4) - 1))
                            pe.wait_ge(probs_made, nth(it, HEADS, h - 2))
                            lo, pair = DH * (step % 2), step // 2
                            for tt in range(TT):
                                last = nc.tensor.matmul(ps_scores[h % 2][:, tt * N:(tt + 1) * N],
                                                        q_T[n % 2][lo:lo + DH, pair, tt * P:(tt + 1) * P],
                                                        k_T[n % 2][lo:lo + DH, pair, :], start=True, stop=True)
                            last.then_inc(scores_made, 1)
                        if 3 <= step < H + 3:
                            h = n * H + step - 3
                            pe.wait_ge(probs_scaled, nth(it, HEADS, h))
                            pe.wait_ge(probs_T_ready, nth(it, HEADS, h - 2))
                            for tt in range(TT):
                                for m in range(TT):
                                    last = nc.tensor.transpose(
                                        ps_probs_T[h % 2][:, m * N + tt * P:m * N + (tt + 1) * P],
                                        probs[h % NP][:, tt, m * P:(m + 1) * P], ident[:])
                            last.then_inc(probs_turned, 1)
                        if 4 <= step:
                            head = step - 4
                            h = n * H + head
                            if head == 0:
                                pe.wait_ge(v_ready, nth(it, QK_CHUNKS // 2, (n + 1) * (QK_CHUNKS // 8) - 1))
                            pe.wait_ge(probs_T_ready, nth(it, HEADS, h))
                            quad = h // 4
                            if head % 4 == 0:
                                pe.wait_ge(o_T_ready, nth(it, QUADS, quad - 2))
                            lo, col = DH * (head % 2), N * (head // 2 % 2)
                            for m in range(TT):
                                last = nc.tensor.matmul(ps_o[quad % 2][lo:lo + DH, col:col + N],
                                                        v[n % 2][:, m, head * DH:(head + 1) * DH],
                                                        probs_T[h % 2][:, m, :], start=(m == 0), stop=(m == TT - 1))
                            last.then_inc(pv_made, 1)


INPUTS = ["x", "cond_1024", "ctx_768"] + [f"L0_xcond_{x}" for x in (
    "ln1_w", "ln1_b", "g1_w", "g1_b", "b1_w", "b1_b", "ln2_w", "ln2_b", "g2_w", "g2_b", "b2_w", "b2_b", "sa_wq",
    "sa_wkv", "sa_wo", "sa_bo", "ca_lnc_w", "ca_lnc_b", "ca_wq", "ca_wkv", "ca_wo", "ca_bo", "ff_w1", "ff_b1",
    "ff_w2", "ff_b2")]


def kernel(**inputs):
    import numpy as np
    import concourse.bacc as bacc
    from concourse.bass_utils import run_bass_kernel_spmd

    inv = (1.0 / 10000.0 ** (np.arange(0, DH, 2, dtype=np.float32) / DH)).astype(np.float32)
    angle = np.arange(N, dtype=np.float32)[:, None] * inv[None, :]
    cos = np.repeat(np.cos(angle), 2, axis=1)
    sin = np.stack((-np.sin(angle), np.sin(angle)), axis=-1).reshape(N, DH)
    scale = np.float32(DH ** -0.5)
    arrays = {"rope_cos_q": cos * scale, "rope_sin_q": sin * scale, "rope_cos_k": cos, "rope_sin_k": sin}
    arrays = {k: np.ascontiguousarray(a.astype(np.float32)) for k, a in arrays.items()}
    for name in INPUTS:
        arrays[name] = np.ascontiguousarray(inputs[name])

    nc = bacc.Bacc("TRN2", target_bir_lowering=False, num_devices=1)
    t = {k: nc.dram_tensor(f"in_{k}", a.shape, mybir.dt.from_np(a.dtype), kind="ExternalInput").ap()
         for k, a in arrays.items()}
    t["out"] = nc.dram_tensor("out_0", (BATCH, N, D), F32, kind="ExternalOutput").ap()
    block_kernel(nc, t)
    r = run_bass_kernel_spmd(nc, [{f"in_{k}": a for k, a in arrays.items()}], core_ids=[0])
    return r.results[0]["out_0"]
```

```python
from contextlib import ExitStack

import concourse.bass as bass
from concourse import mybir

F32 = mybir.dt.float32
F16 = mybir.dt.float16
ALU = mybir.AluOpType
ACT = mybir.ActivationFunctionType
AX = mybir.AxisListType

P = 128
BATCH, N, D = 16, 256, 256
H, DH = 16, 64
MID = H * DH
DC = 192
FF = 4 * D
EPS = 1e-5
TT = N // P
KT = D // P
CHUNK = 512
HALVES = MID // CHUNK
CH_HEADS = CHUNK // DH
PAIRS = H // 2
MT = MID // P
SLOTS = 2
ITERS = BATCH // SLOTS
TURN_LAG = 4
PV_LAG = 5
LAST_STEP = H + PV_LAG
W_SCALE = 64.0

PASSES = [("self", 0), ("self", 1), ("cross", 0), ("cross", 1)]


def projection_units(n):
    chunks = [("chunk", n, x, tt, half) for tt in range(TT) for x in "qkv" for half in range(HALVES)]
    units, late = [], []
    for i, c in enumerate(chunks + [None] * 3):
        units += [u for at, u in late if at == i]
        if c:
            units.append(("bank", c))
            if c[2] != "v":
                late += [(i + 1, ("high", c)), (i + 2, ("low", c))]
                late += [(i + 3, ("bank", ("turn", n, x) + c[3:])) for x in (["q", "q_low"] if c[2] == "q" else ["k"])]
    return units


def make_schedule():
    s = [("stats", ("ln", 0)), ("norm", ("ln", 0)), ("bank", ("lnT", ("ln", 0)))]
    s += projection_units(0)
    for n in range(len(PASSES)):
        after = [[] for _ in range(LAST_STEP)]
        if n:
            after[1].append(("bank", ("wo", n - 1)))
        following = ("ln", n + 1) if n < 3 else ("ff", 0)
        after[1].append(("stats", following))
        after[2].append(("norm", following))
        after[3].append(("bank", ("lnT", following)))
        if n < 3:
            if PASSES[n + 1][0] == "cross":
                after[2].append(("stats", ("ctx", n + 1)))
                after[3].append(("norm", ("ctx", n + 1)))
                after[4].append(("bank", ("lnT", ("ctx", n + 1))))
            units = projection_units(n + 1)
            for i, u in enumerate(units):
                after[4 + i * (LAST_STEP - 5) // len(units)].append(u)
        for step in range(LAST_STEP):
            s.append(("step", (n, step)))
            s += after[step]
    s += [("bank", ("hidden", 0, j)) for j in range(FF // P // 2)]
    s += [("bank", ("wo", 3)), ("stats", ("ff", 1)), ("bank", ("out", 0)), ("store", 0), ("norm", ("ff", 1)),
          ("bank", ("lnT", ("ff", 1)))]
    s += [("bank", ("hidden", 1, j)) for j in range(FF // P // 2)]
    s += [("bank", ("out", 1)), ("store", 1)]
    return s


SCHEDULE = make_schedule()
BANK_USES = [x for kind, x in SCHEDULE if kind == "bank"]
NORMS = [x for kind, x in SCHEDULE if kind == "stats"]
RESIDUALS = [x for x in BANK_USES if x[0] in ("wo", "out")]
Q_TURNS = [x for x in BANK_USES if x[0] == "turn" and x[2] != "k"]
K_TURNS = [x for x in BANK_USES if x[0] == "turn" and x[2] == "k"]
V_CHUNKS = [x for x in BANK_USES if x[0] == "chunk" and x[2] == "v"]
HIDDENS = [x for x in BANK_USES if x[0] == "hidden"]
assert len(BANK_USES) % 2 == 0, len(BANK_USES)

VECTOR_LOADS = 3 + 10 * KT + 1


def vector_loads(t, bias_row, vec, ff_b1):
    for x, name in (("self", "sa_bo"), ("cross", "ca_bo"), ("ff", "ff_b2")):
        yield bias_row[x][:], t[f"L0_xcond_{name}"].unsqueeze(0).broadcast_to([P, D])
    for x, dst in vec.items():
        src = t[f"L0_xcond_{x}"].unsqueeze(1)
        for k, (col, rows) in enumerate([(0, P), (P, DC - P if x.startswith("ca") else P)]):
            yield dst[0:rows, k:k + 1], src[col:col + rows, :]
    yield ff_b1[:], t["L0_xcond_ff_b1"].rearrange("(t p) -> p t", p=P)


def block_kernel(nc, t):
    with ExitStack() as ctx:
        def sb(name, shape, dt=F32):
            return ctx.enter_context(nc.sbuf_tensor(name, shape, dt))

        def pb(name):
            return ctx.enter_context(nc.psum_tensor(name, [P, 512], F32))

        def sem(name):
            return ctx.enter_context(nc.semaphore(name))

        def parts(name, shape):
            return [sb(f"{name}_{part}", shape, F16) for part in ("high", "low")]

        w_q = {"self": parts("w_sa_q", [P, KT, MID]), "cross": parts("w_ca_q", [P, KT, MID])}
        w_kv = {"self": parts("w_sa_kv", [P, KT, 2 * MID]), "cross": parts("w_ca_kv", [P, KT, 2 * MID])}
        w_o = {"self": parts("w_sa_o", [P, MT, D]), "cross": parts("w_ca_o", [P, MT, D])}
        w_1 = parts("w_1", [P, KT, FF])
        w_2 = parts("w_2", [P, FF // P, D])
        bias_row = {x: sb(f"bias_{x}", [P, D]) for x in ("self", "cross", "ff")}
        vec = {x: sb(f"vec_{x}", [P, KT]) for x in (
            "ln1_w", "ln1_b", "g1_b", "b1_b", "ln2_w", "ln2_b", "g2_b", "b2_b", "ca_lnc_w", "ca_lnc_b")}
        ff_b1 = sb("ff_b1", [P, FF // P])
        rope_cos = {x: sb(f"rope_cos_{x}", [P, TT, DH // 2]) for x in "qk"}
        rope_sin = {x: sb(f"rope_sin_{x}", [P, TT, DH]) for x in "qk"}
        ident = sb("ident", [P, P])
        ident_16 = sb("ident_16", [P, P], F16)
        minus_half = sb("minus_half", [P, TT])
        gain = {x: sb(f"gain_{x}", [P, KT, BATCH]) for x in ("1", "2")}
        shift = {x: sb(f"shift_{x}", [P, KT, BATCH]) for x in ("1", "2")}

        x_in = [sb(f"x_in{s}", [P, TT, D]) for s in range(SLOTS)]
        c_in = [sb(f"c_in{s}", [P, TT, DC]) for s in range(SLOTS)]
        x_res = [sb(f"x_res{s}", [P, TT, D]) for s in range(SLOTS)]
        stats = [sb(f"stats{i}", [P, TT, 6]) for i in range(2)]
        moments = [sb(f"moments{i}", [P, TT, 2]) for i in range(2)]
        var_eps = [sb(f"var_eps{i}", [P, TT]) for i in range(2)]
        rstd = [sb(f"rstd{i}", [P, TT]) for i in range(2)]
        x_hat = sb("x_hat", [P, TT, D])
        y_T = sb("y_T", [P, KT, N])
        a_T = parts("a_T", [P, KT, N])
        c_T = parts("c_T", [P, KT, N])
        x_cos = [sb(f"x_cos{i}", [P, CHUNK]) for i in range(2)]
        x_sin = [sb(f"x_sin{i}", [P, CHUNK]) for i in range(2)]
        roped = [sb(f"roped{i}", [P, CHUNK]) for i in range(2)]
        roped_parts = [sb(f"roped_parts{i}", [P, 3 * CHUNK], F16) for i in range(2)]
        turned_parts = {x: [sb(f"{x}_T{i}", [P, heads, N], F16) for i in range(2)]
                        for x, heads in (("q", H), ("k", H), ("q_low", PAIRS))}
        o_T = parts("o_T", [P, PAIRS, N])
        gelu = x_cos
        h_T = [turned_parts["q"][0][:, i * (FF // P):(i + 1) * (FF // P), :] for i in range(2)]
        w_cond = {x: turned_parts["q"][1][:].rearrange("p a n -> p (a n)").bitcast(F32)[
            :, i * KT * D:(i + 1) * KT * D].rearrange("p (t n) -> p t n", t=KT)
            for i, x in enumerate(("g1", "b1", "g2", "b2"))}
        v = [sb(f"v{i}", [P, TT, MID]) for i in range(2)]
        NP = 5
        staging = [v[0][:].rearrange("p t n -> p (t n)"), v[1][:].rearrange("p t n -> p (t n)")] + [
            turned_parts[x][i][:].rearrange("p a n -> p (a n)").bitcast(F32) for x, i in (("k", 0), ("k", 1))]
        probs = [sb(f"probs{i}", [P, TT, N]) for i in range(NP)]
        cond = probs[0][0:BATCH, 0, :]
        cond_T = probs[1][:, 0, 0:KT * BATCH].rearrange("p (t b) -> p t b", t=KT)
        one_plus_g = probs[2][:, 0, 0:2 * KT * BATCH].rearrange("p (i t b) -> p i t b", i=2, t=KT)
        probs_T = [sb(f"probs_T{i}", [P, TT, N]) for i in range(2)]
        neg_max = sb("neg_max", [P, NP, TT])
        row_sum = sb("row_sum", [P, NP, TT])
        row_inv = sb("row_inv", [P, NP, TT])

        def slab(name, hl, k=None, first=0, rows=P):
            src = t[f"L0_xcond_{name}"]
            if k is not None:
                return src[first:first + rows, :], [w[0:rows, k, :] for w in hl], rows
            return (src.rearrange("(t p) n -> p t n", p=P), [w[:].rearrange("p t n -> p (t n)") for w in hl], rows)

        SLABS = [slab("sa_wq", w_q["self"]), slab("sa_wkv", w_kv["self"], 0, 0), slab("sa_wkv", w_kv["self"], 1, P),
                 slab("sa_wo", w_o["self"]), slab("ca_wq", w_q["cross"]), slab("ca_wkv", w_kv["cross"], 0, 0),
                 slab("ca_wkv", w_kv["cross"], 1, P, DC - P), slab("ca_wo", w_o["cross"]), slab("ff_w1", w_1),
                 slab("ff_w2", w_2)]
        SPLIT = {("q", "self"): 1, ("k", "self"): 3, ("wo", "self"): 4, ("q", "cross"): 5, ("k", "cross"): 7,
                 ("wo", "cross"): 8, "ff_w1": 9, "ff_w2": 10}

        bank = [pb("bank0"), pb("bank1")]
        ps_scores = [pb("ps_scores0"), pb("ps_scores1")]
        ps_probs_T = [pb("ps_probs_T0"), pb("ps_probs_T1")]
        ps_o = [pb("ps_o0"), pb("ps_o1")]

        vectors_loaded, rope_loaded, cond_loaded = sem("vectors_loaded"), sem("rope_loaded"), sem("cond_loaded")
        slab_loaded = [sem(f"slab_loaded{i}") for i in range(len(staging))]
        w_high_made, w_split = sem("w_high_made"), sem("w_split")
        x_loaded = [sem(f"x_loaded{s}") for s in range(SLOTS)]
        c_loaded = [sem(f"c_loaded{s}") for s in range(SLOTS)]
        stored = [sem(f"stored{s}") for s in range(SLOTS)]
        ident_made = sem("ident_made")
        cond_turned, cond_copied, cond_projected, cond_ready = (
            sem("cond_turned"), sem("cond_copied"), sem("cond_projected"), sem("cond_ready"))
        bank_filled = sem("bank_filled")
        stats_made, moments_made, var_made, rstd_made, x_hat_made = (
            sem("stats_made"), sem("moments_made"), sem("var_made"), sem("rstd_made"), sem("x_hat_made"))
        a_T_ready = sem("a_T_ready")
        biased_made, residual_made = sem("biased_made"), sem("residual_made")
        y_T_made, a_high_made = sem("y_T_made"), sem("a_high_made")
        parts_made, roped_made, roped_high, roped_low = (
            sem("parts_made"), sem("roped_made"), sem("roped_high"), sem("roped_low"))
        q_T_ready, k_T_ready, v_ready = sem("q_T_ready"), sem("k_T_ready"), sem("v_ready")
        scores_made, max_made, probs_made, inv_made, probs_scaled = (
            sem("scores_made"), sem("max_made"), sem("probs_made"), sem("inv_made"), sem("probs_scaled"))
        probs_turned, probs_T_ready, pv_made, o_T_ready = (
            sem("probs_turned"), sem("probs_T_ready"), sem("pv_made"), sem("o_T_ready"))
        o_high_made, gelu_made, hidden_high, hidden_ready = (
            sem("o_high_made"), sem("gelu_made"), sem("hidden_high"), sem("hidden_ready"))
        sp_passed, dve_passed = sem("sp_passed"), sem("dve_passed")

        CREDIT = 32
        credited = [*x_loaded, *c_loaded, *stored, bank_filled, stats_made, moments_made, var_made, rstd_made,
                    x_hat_made, y_T_made, a_high_made, a_T_ready, biased_made, residual_made, parts_made, roped_made,
                    roped_high, roped_low, q_T_ready, k_T_ready, v_ready, scores_made, max_made, probs_made, inv_made,
                    probs_scaled, probs_turned, probs_T_ready, pv_made, o_high_made, o_T_ready, gelu_made,
                    hidden_high, hidden_ready]

        def nth(it, per_iteration, ordinal):
            return it * per_iteration + (ordinal + 1 + CREDIT)

        def nth_dma(it):
            return it * 16 + (16 + CREDIT)

        def chunk_no(u):
            _, n, x, tt, half = u
            return ((n * TT + tt) * 2 + "qk".index(x[0])) * HALVES + half

        LAST_TURNS = sorted([x for x in BANK_USES if x[0] == "turn" and x[2] != "q"], key=chunk_no)
        QK_CHUNKS = len(PASSES) * TT * 2 * HALVES
        HEADS = len(PASSES) * H
        QUADS = HEADS // 4

        def bank_of(w):
            return bank[w % 2]

        def turned(it, things, i):
            if i < 0:
                it, i = it - 1, i + len(things)
            return nth(it, len(BANK_USES), BANK_USES.index(things[i]))

        def emptied(it, w):
            if w < 0:
                it, w = it - 1, w + len(BANK_USES)
            u = BANK_USES[w]
            if u[0] == "lnT":
                return y_T_made, nth(it, len(NORMS), NORMS.index(u[1]))
            if u[0] == "turn":
                if u[2] != "k":
                    return q_T_ready, nth(it, len(Q_TURNS), Q_TURNS.index(u))
                return k_T_ready, nth(it, len(K_TURNS), K_TURNS.index(u))
            if u[0] == "hidden":
                return gelu_made, nth(it, len(HIDDENS), HIDDENS.index(u))
            if u[0] in ("wo", "out"):
                return residual_made, nth(it, len(RESIDUALS), RESIDUALS.index(u))
            if u[2] == "v":
                return v_ready, nth(it, QK_CHUNKS // 2, V_CHUNKS.index(u))
            return parts_made, nth(it, QK_CHUNKS, chunk_no(u))

        def high_of(x, c):
            if x == "q":
                return roped_parts[c % 2][:, 0:2 * CHUNK].rearrange("p (a two c d) -> p a two c d", two=2, c=2, d=DH)
            return roped_parts[c % 2][:, 0:2 * CHUNK].rearrange("p (a four c d) -> p a four c d", four=4, c=1, d=DH)[
                :, :, 0:4:3]

        def low_of(x, c):
            if x == "q":
                return roped_parts[c % 2][:, 2 * CHUNK:3 * CHUNK].rearrange("p (a two d) -> p a two d", two=2, d=DH)
            return roped_parts[c % 2][:, 0:2 * CHUNK].rearrange("p (a four d) -> p a four d", four=4, d=DH)[:, :, 1:3]

        def source(x):
            kind, n = x
            if kind == "ctx":
                return c_in[PASSES[n][1]]
            if kind == "ff":
                return x_res[n]
            return x_in[n] if n < 2 else x_res[n - 2]

        def quad_of(n, step):
            q, r = divmod(step - PV_LAG - 4, 4)
            if step == LAST_STEP - 1:
                q, r = 3, 0
            return 4 * n + q if r == 0 and 0 <= q < 4 else None

        def stream(u):
            kind, n = u
            slot = n % 2
            return (x_in if kind == "wo" and n < 2 else x_res)[slot], x_res[slot]

        def widths(kind):
            return [(0, P), (P, DC - P)] if kind == "ctx" else [(0, P), (P, P)]

        block = ctx.enter_context(nc.Block())

        @block.sync
        def _(sp):
            def load(dst, src, s):
                sp.dma_start(dst, src).then_inc(s, 16)

            def load_x(b, s):
                sp.dma_start(x_in[s][:], t["x"][bass.ds(b, 1), :, :].rearrange(
                    "b (t p) d -> p (b t) d", p=P)).then_inc(x_loaded[s], 16)

            def load_c(b, s):
                sp.dma_start(c_in[s][:], t["ctx_768"][bass.ds(b, 1), :, :].rearrange(
                    "b (t p) d -> p (b t) d", p=P)).then_inc(c_loaded[s], 16)

            load_x(0, 0)
            load(cond, t["cond_1024"], cond_loaded)
            for x in ("g1", "b1", "g2", "b2"):
                load(w_cond[x], t[f"L0_xcond_{x}_w"].rearrange("(t p) n -> p t n", p=P), cond_loaded)
            for i, (src, _, rows) in enumerate(SLABS):
                j = i % len(staging)
                if i >= len(staging):
                    sp.wait_ge(w_split, i - len(staging) + 1)
                dst = staging[j][0:rows, :]
                if len(src.shape) == 3:
                    dst = dst.rearrange("p (t n) -> p t n", t=src.shape[1])
                load(dst, src, slab_loaded[j])
                if i == 2:
                    load_x(1, 1)
                    load_c(0, 0)
                    load_c(1, 1)
            with sp.Fori(1, ITERS) as it:
                for s in range(SLOTS):
                    sp.wait_ge(residual_made, nth(it - 1, len(RESIDUALS), s))
                    sp.sem_inc(sp_passed, 1)
                    load_x(it * SLOTS + s, s)
                for s in range(SLOTS):
                    sp.wait_ge(x_hat_made, nth(it - 1, len(NORMS), NORMS.index(("ctx", 2 + s))))
                    sp.sem_inc(sp_passed, 1)
                    load_c(it * SLOTS + s, s)

        @block.gpsimd
        def _(pool):
            for s in credited:
                pool.sem_inc(s, CREDIT)
            nc.gpsimd.memset(minus_half[:], -0.5)
            nc.gpsimd.memset(ident[:], 0.0).then_inc(ident_made, 1)
            pool.wait_ge(ident_made, 1)
            nc.gpsimd.affine_select(out=ident[:], in_=ident[:], compare_op=ALU.not_equal, fill=1.0, base=0,
                                    pattern=[[-1, P]], channel_multiplier=1).then_inc(ident_made, 1)
            pool.wait_ge(ident_made, 2)
            nc.gpsimd.tensor_copy(ident_16[:], ident[:]).then_inc(ident_made, 1)
            pool.wait_ge(vectors_loaded, 16 * VECTOR_LOADS)

            def add_bias(it, x):
                kind, n = x
                r = RESIDUALS.index(("out" if kind == "ff" else "wo", n))
                src = stream(RESIDUALS[r])[0]
                pool.wait_ge(x_hat_made, nth(it, len(NORMS), NORMS.index(x)))
                row = bias_row["ff" if kind == "ff" else PASSES[n][0]]
                nc.gpsimd.tensor_tensor(out=src[:], in0=src[:], in1=row[:].unsqueeze(1).broadcast_to([P, TT, D]),
                                        op=ALU.add).then_inc(biased_made, 1)

            with pool.Fori(0, ITERS) as it:
                for kind, x in SCHEDULE:
                    if kind == "stats":
                        n = NORMS.index(x)
                        pool.wait_ge(var_made, nth(it, len(NORMS), n))
                        nc.gpsimd.tensor_tensor(out=rstd[n % 2][:], in0=var_eps[n % 2][:], in1=minus_half[:],
                                                op=ALU.pow).then_inc(rstd_made, 1)
                    elif kind == "bank" and x[0] == "chunk" and x[2] != "v":
                        c = chunk_no(x)
                        pool.wait_ge(parts_made, nth(it, QK_CHUNKS, c))
                        pool.wait_ge(roped_low, nth(it, QK_CHUNKS, c - 2))
                        nc.gpsimd.tensor_tensor(out=roped[c % 2][:], in0=x_cos[c % 2][:], in1=x_sin[c % 2][:],
                                                op=ALU.add).then_inc(roped_made, 1)
                    elif kind == "low":
                        c = chunk_no(x)
                        pool.wait_ge(roped_high, nth(it, QK_CHUNKS, c))
                        nc.gpsimd.tensor_tensor(out=low_of(x[2], c),
                                                in0=roped[c % 2][:].rearrange("p (a two d) -> p a two d", two=2, d=DH),
                                                in1=high_of(x[2], c)[:, :, :, 0, :], op=ALU.subtract).then_inc(roped_low, 1)
                    elif kind == "bank" and x[0] == "lnT" and x[1][0] != "ctx":
                        add_bias(it, x[1])
                    elif kind == "step":
                        n, step = x
                        if 1 <= step <= H:
                            h = n * H + step - 1
                            pool.wait_ge(inv_made, nth(it, HEADS, h))
                            nc.gpsimd.tensor_tensor(
                                out=probs[h % NP][:], in0=probs[h % NP][:],
                                in1=row_inv[:, h % NP, :].unsqueeze(2).broadcast_to([P, TT, N]),
                                op=ALU.mult).then_inc(probs_scaled, 1)

        @block.vector
        def _(dve):
            def condition():
                dve.wait_ge(cond_turned, 1)
                nc.vector.tensor_copy(cond_T, bank[0][:, 0:KT * BATCH].rearrange(
                    "p (t b) -> p t b", t=KT)).then_inc(cond_copied, 1)
                dve.wait_ge(vectors_loaded, 16 * VECTOR_LOADS)
                dve.wait_ge(cond_projected, 1)
                made = bank[1][:, 0:4 * KT * BATCH].rearrange("p (m t b) -> p m t b", m=4, t=KT)
                for i, x in enumerate("12"):
                    for k in range(KT):
                        nc.vector.tensor_scalar(one_plus_g[:, i, k, :], made[:, 2 * i, k, :], vec[f"g{x}_b"][:, k:k + 1],
                                                1.0, ALU.add, ALU.add)
                        last = nc.vector.tensor_scalar(shift[x][:, k, :], made[:, 2 * i + 1, k, :],
                                                       vec[f"b{x}_b"][:, k:k + 1], None, ALU.add)
                last.then_inc(cond_ready, 1)
                dve.wait_ge(cond_ready, 1)
                for i, x in enumerate("12"):
                    for k in range(KT):
                        nc.vector.tensor_scalar(gain[x][:, k, :], one_plus_g[:, i, k, :], vec[f"ln{x}_w"][:, k:k + 1],
                                                None, ALU.mult)
                        last = nc.vector.scalar_tensor_tensor(
                            out=shift[x][:, k, :], in0=one_plus_g[:, i, k, :], scalar=vec[f"ln{x}_b"][:, k:k + 1],
                            in1=shift[x][:, k, :], op0=ALU.mult, op1=ALU.add)
                last.then_inc(cond_ready, 1)

            for i, (_, (high, low), rows) in enumerate(SLABS):
                dve.wait_ge(w_high_made, i + 1)
                nc.vector.scalar_tensor_tensor(out=low, in0=staging[i % len(staging)][0:rows, :], scalar=W_SCALE,
                                               in1=high, op0=ALU.mult, op1=ALU.subtract).then_inc(w_split, 1)
                if i == 0:
                    condition()
            dve.wait_ge(rope_loaded, 16 * 4)
            dve.wait_ge(cond_ready, 2)

            def layernorm_stats(it, n):
                kind, at = NORMS[n]
                src, j = source(NORMS[n]), n % 2
                if kind == "ctx":
                    dve.wait_ge(c_loaded[PASSES[at][1]], nth_dma(it))
                elif kind == "ln" and at < 2:
                    dve.wait_ge(x_loaded[at], nth_dma(it))
                else:
                    r = RESIDUALS.index(("wo", at - 2 if kind == "ln" else at + 2))
                    dve.wait_ge(residual_made, nth(it, len(RESIDUALS), r))
                dve.wait_ge(x_hat_made, nth(it, len(NORMS), n - 2))
                for tt in range(TT):
                    last = nc.vector.bn_stats(out=stats[j][:, tt, :], in_=src[:, tt, :])
                last.then_inc(stats_made, 1)
                dve.wait_ge(stats_made, nth(it, len(NORMS), n))
                dve.sem_inc(dve_passed, 1)
                for tt in range(TT):
                    last = nc.vector.bn_aggr(out=moments[j][:, tt, :], in_=stats[j][:, tt, :])
                last.then_inc(moments_made, 1)
                dve.wait_ge(moments_made, nth(it, len(NORMS), n))
                nc.vector.tensor_scalar(var_eps[j][:], moments[j][:, :, 1], EPS, None, ALU.add).then_inc(var_made, 1)

            def layernorm_apply(it, n):
                src, j = source(NORMS[n]), n % 2
                width = DC if NORMS[n][0] == "ctx" else D
                dve.wait_ge(rstd_made, nth(it, len(NORMS), n))
                dve.wait_ge(bank_filled, turned(it, [("lnT", x) for x in NORMS], n - 1))
                for tt in range(TT):
                    last = nc.vector.tensor_scalar(x_hat[:, tt, 0:width], src[:, tt, :], moments[j][:, tt, 0:1],
                                                   rstd[j][:, tt:tt + 1], ALU.subtract, ALU.mult)
                last.then_inc(x_hat_made, 1)

            def empty_bank(it, w):
                u = BANK_USES[w]
                src = bank_of(w)
                if u[0] == "lnT":
                    kind, at = u[1]
                    dve.wait_ge(bank_filled, nth(it, len(BANK_USES), w))
                    i = NORMS.index(u[1])
                    high, low = c_T if kind == "ctx" else a_T
                    for k, (_, rows) in enumerate(widths(kind)):
                        if kind == "ctx":
                            g, b = vec["ca_lnc_w"][0:rows, k:k + 1], vec["ca_lnc_b"][0:rows, k:k + 1]
                        else:
                            which = "2" if kind == "ff" else "1"
                            s = at if kind == "ff" else PASSES[at][1]
                            g = gain[which][:, k, bass.ds(it * SLOTS + s, 1)]
                            b = shift[which][:, k, bass.ds(it * SLOTS + s, 1)]
                        last = nc.vector.tensor_scalar(y_T[0:rows, k, :], src[0:rows, k * N:(k + 1) * N], g, b,
                                                       ALU.mult, ALU.add)
                    last.then_inc(y_T_made, 1)
                    dve.wait_ge(y_T_made, nth(it, len(NORMS), i))
                    for k, (_, rows) in enumerate(widths(kind)):
                        last = nc.vector.tensor_copy(high[0:rows, k, :], y_T[0:rows, k, :])
                    last.then_inc(a_high_made, 1)
                    dve.wait_ge(a_high_made, nth(it, len(NORMS), i))
                    for k, (_, rows) in enumerate(widths(kind)):
                        last = nc.vector.tensor_tensor(out=low[0:rows, k, :], in0=y_T[0:rows, k, :],
                                                       in1=high[0:rows, k, :], op=ALU.subtract)
                    last.then_inc(a_T_ready, 1)
                elif u[0] == "turn" and u[2] != "k":
                    _, n, x, tt, half = u
                    heads = CH_HEADS // (2 if x == "q_low" else 1)
                    dve.wait_ge(bank_filled, nth(it, len(BANK_USES), w))
                    nc.vector.tensor_copy(
                        turned_parts[x][n % 2][:, half * heads:(half + 1) * heads, tt * P:(tt + 1) * P],
                        src[:].bitcast(F16)[:, 0:heads * P].rearrange("p (h n) -> p h n", h=heads)).then_inc(q_T_ready, 1)
                elif u[0] == "hidden":
                    j = HIDDENS.index(u)
                    dve.wait_ge(hidden_high, nth(it, len(HIDDENS), j))
                    m = 2 * u[2]
                    nc.vector.tensor_tensor(out=h_T[1][:, m:m + 2, :].rearrange("p m n -> p (m n)"),
                                            in0=gelu[j % 2][:], in1=h_T[0][:, m:m + 2, :].rearrange("p m n -> p (m n)"),
                                            op=ALU.subtract).then_inc(hidden_ready, 1)
                elif u[0] == "chunk" and u[2] != "v":
                    _, n, x, tt, half = u
                    c = chunk_no(u)
                    dve.wait_ge(bank_filled, nth(it, len(BANK_USES), w))
                    dve.wait_ge(roped_made, nth(it, QK_CHUNKS, c - 2))
                    pairs = "p (h j two) -> p h j two"
                    cos = rope_cos[x][:, tt, :].unsqueeze(1).unsqueeze(3).broadcast_to([P, CH_HEADS, DH // 2, 2])
                    nc.vector.tensor_tensor(out=x_cos[c % 2][:].rearrange(pairs, two=2, j=DH // 2),
                                            in0=src[:].rearrange(pairs, two=2, j=DH // 2), in1=cos, op=ALU.mult)
                    sin = rope_sin[x][:, tt, :].rearrange("p (j two) -> p j two", two=2)
                    sin = sin.unsqueeze(1).broadcast_to([P, CH_HEADS, DH // 2, 2])
                    nc.vector.tensor_tensor(out=x_sin[c % 2][:].rearrange(pairs, two=2, j=DH // 2),
                                            in0=src[:].rearrange(pairs, two=2, j=DH // 2)[:, :, :, ::-1],
                                            in1=sin, op=ALU.mult).then_inc(parts_made, 1)
                elif u[0] in ("wo", "out"):
                    r = RESIDUALS.index(u)
                    dve.wait_ge(bank_filled, nth(it, len(BANK_USES), w))
                    dve.wait_ge(biased_made, nth(it, len(RESIDUALS), r))
                    if u[0] == "wo" and u[1] < 2:
                        dve.wait_ge(stored[u[1]], nth_dma(it - 1))
                    before, after = stream(u)
                    flat = "p t d -> p (t d)"
                    nc.vector.scalar_tensor_tensor(out=after[:].rearrange(flat), in0=src[:], scalar=1.0 / W_SCALE,
                                                   in1=before[:].rearrange(flat), op0=ALU.mult,
                                                   op1=ALU.add).then_inc(residual_made, 1)

            with dve.Fori(0, ITERS) as it:
                for kind, x in SCHEDULE:
                    if kind == "stats":
                        layernorm_stats(it, NORMS.index(x))
                    elif kind == "norm":
                        layernorm_apply(it, NORMS.index(x))
                    elif kind == "bank":
                        empty_bank(it, BANK_USES.index(x))
                    elif kind == "step":
                        n, step = x
                        if step < H:
                            h = n * H + step
                            dve.wait_ge(scores_made, nth(it, HEADS, h))
                            nc.vector.tensor_reduce(
                                out=neg_max[:, h % NP, :], in_=ps_scores[h % 2][:].rearrange("p (t m) -> p t m", t=TT),
                                axis=AX.X, op=ALU.max, negate=True).then_inc(max_made, 1)
                        if 1 <= step <= H:
                            h = n * H + step - 1
                            dve.wait_ge(probs_made, nth(it, HEADS, h))
                            nc.vector.reciprocal(row_inv[:, h % NP, :], row_sum[:, h % NP, :]).then_inc(inv_made, 1)
                        if TURN_LAG <= step < H + TURN_LAG:
                            h = n * H + step - TURN_LAG
                            dve.wait_ge(probs_turned, nth(it, HEADS, h))
                            dve.wait_ge(pv_made, nth(it, HEADS, h - 2))
                            nc.vector.tensor_copy(probs_T[h % 2][:].rearrange("p t n -> p (t n)"),
                                                  ps_probs_T[h % 2][:]).then_inc(probs_T_ready, 1)
                        if (quad := quad_of(n, step)) is not None:
                            q = quad % 4
                            dve.wait_ge(o_high_made, nth(it, QUADS, quad))
                            high, low = [o[:, 2 * q:2 * q + 2, :].rearrange("p a n -> p (a n)") for o in o_T]
                            nc.vector.tensor_tensor(out=low, in0=ps_o[quad % 2][:], in1=high,
                                                    op=ALU.subtract).then_inc(o_T_ready, 1)

        @block.scalar
        def _(act):
            for dst, src in vector_loads(t, bias_row, vec, ff_b1):
                act.dma_start(dst, src, allow_slow_non_contiguous=True).then_inc(vectors_loaded, 16)
            for x in "qk":
                act.dma_start(rope_cos[x][:], t[f"rope_cos_{x}"].rearrange("(t p) d -> p t d", p=P)).then_inc(rope_loaded, 16)
                act.dma_start(rope_sin[x][:], t[f"rope_sin_{x}"].rearrange("(t p) d -> p t d", p=P)).then_inc(rope_loaded, 16)
            for i, (_, (high, low), rows) in enumerate(SLABS):
                act.wait_ge(slab_loaded[i % len(staging)], 16 * (i // len(staging) + 1))
                nc.scalar.activation(high, staging[i % len(staging)][0:rows, :], ACT.Copy,
                                     scale=W_SCALE).then_inc(w_high_made, 1)

            def empty_bank(it, w):
                u = BANK_USES[w]
                src = bank_of(w)
                if u[0] == "turn" and u[2] == "k":
                    _, n, x, tt, half = u
                    act.wait_ge(bank_filled, nth(it, len(BANK_USES), w))
                    nc.scalar.activation(
                        turned_parts[x][n % 2][:, half * CH_HEADS:(half + 1) * CH_HEADS, tt * P:(tt + 1) * P],
                        src[:].bitcast(F16).rearrange("p (h n) -> p h n", h=CH_HEADS),
                        ACT.Copy).then_inc(k_T_ready, 1)
                elif u[0] == "chunk" and u[2] == "v":
                    _, n, x, tt, half = u
                    act.wait_ge(bank_filled, nth(it, len(BANK_USES), w))
                    nc.scalar.activation(v[n % 2][:, tt, half * CHUNK:(half + 1) * CHUNK], src[:],
                                         ACT.Copy, scale=1.0 / W_SCALE).then_inc(v_ready, 1)
                elif u[0] == "hidden":
                    j = HIDDENS.index(u)
                    m = 2 * u[2]
                    act.wait_ge(bank_filled, nth(it, len(BANK_USES), w))
                    act.wait_ge(hidden_ready, nth(it, len(HIDDENS), j - 2))
                    for i in range(2):
                        last = nc.scalar.activation(gelu[j % 2][:, i * N:(i + 1) * N], src[:, i * N:(i + 1) * N],
                                                    ACT.Gelu, bias=ff_b1[:, m + i:m + i + 1], scale=1.0 / W_SCALE)
                    last.then_inc(gelu_made, 1)
                    act.wait_ge(gelu_made, nth(it, len(HIDDENS), j))
                    nc.scalar.activation(h_T[0][:, m:m + 2, :].rearrange("p m n -> p (m n)"), gelu[j % 2][:],
                                         ACT.Copy).then_inc(hidden_high, 1)

            act.wait_ge(vectors_loaded, 16 * VECTOR_LOADS)
            act.wait_ge(w_split, len(SLABS))
            with act.Fori(0, ITERS) as it:
                for kind, x in SCHEDULE:
                    if kind == "bank":
                        empty_bank(it, BANK_USES.index(x))
                    elif kind == "high":
                        c = chunk_no(x)
                        act.wait_ge(roped_made, nth(it, QK_CHUNKS, c))
                        act.wait_ge(bank_filled, turned(it, LAST_TURNS, c - 2))
                        high = high_of(x[2], c)
                        src = roped[c % 2][:].rearrange("p (a two d) -> p a two d", two=2, d=DH)
                        if x[2] == "q":
                            src = src.unsqueeze(3).broadcast_to(list(high.shape)).rearrange("p a two c d -> p (a two) c d")
                            high = high.rearrange("p a two c d -> p (a two) c d")
                        else:
                            high = high[:, :, :, 0, :]
                        nc.scalar.activation(high, src, ACT.Copy).then_inc(roped_high, 1)
                    elif kind == "store":
                        act.wait_ge(residual_made, nth(it, len(RESIDUALS), RESIDUALS.index(("out", x))))
                        act.dma_start(t["out"][bass.ds(it * SLOTS + x, 1), :, :].rearrange("b (t p) d -> p (b t) d", p=P),
                                      x_res[x][:]).then_inc(stored[x], 16)
                    elif kind == "step":
                        n, step = x
                        if step < H:
                            h = n * H + step
                            act.wait_ge(max_made, nth(it, HEADS, h))
                            act.wait_ge(probs_turned, nth(it, HEADS, h - NP))
                            for tt in range(TT):
                                last = nc.scalar.activation(probs[h % NP][:, tt, :], ps_scores[h % 2][:, tt * N:(tt + 1) * N],
                                                            ACT.Exp, bias=neg_max[:, h % NP, tt:tt + 1],
                                                            accum_out=row_sum[:, h % NP, tt:tt + 1])
                            last.then_inc(probs_made, 1)
                        if (quad := quad_of(n, step)) is not None:
                            act.wait_ge(pv_made, nth(it, HEADS, 4 * quad + 3))
                            q = quad % 4
                            nc.scalar.activation(o_T[0][:, 2 * q:2 * q + 2, :].rearrange("p a n -> p (a n)"),
                                                 ps_o[quad % 2][:], ACT.Copy).then_inc(o_high_made, 1)
            for s in range(SLOTS):
                act.wait_ge(stored[s], CREDIT + 16 * ITERS)

        @block.tensor
        def _(pe):
            pe.wait_ge(ident_made, 3)
            pe.wait_ge(cond_loaded, 16 * 5)
            for k in range(KT):
                last = nc.tensor.transpose(bank[0][:, k * BATCH:(k + 1) * BATCH], cond[:, k * P:(k + 1) * P],
                                           ident[0:BATCH, 0:BATCH])
            last.then_inc(cond_turned, 1)
            pe.wait_ge(cond_copied, 1)
            for m, x in enumerate(("g1", "b1", "g2", "b2")):
                for dt in range(KT):
                    col = (m * KT + dt) * BATCH
                    for k in range(KT):
                        last = nc.tensor.matmul(bank[1][:, col:col + BATCH], w_cond[x][:, k, dt * P:(dt + 1) * P],
                                                cond_T[:, k, :], start=(k == 0), stop=(k == KT - 1))
            last.then_inc(cond_projected, 1)
            pe.wait_ge(cond_ready, 1)

            def product(dst, stationary, moving, first, last):
                terms = ((0, 0), (0, 1), (1, 0))
                for i, (a, b) in enumerate(terms):
                    mm = nc.tensor.matmul(dst, stationary[a], moving[b], start=first and i == 0,
                                          stop=last and i == len(terms) - 1)
                return mm

            def fill_bank(it, w):
                u = BANK_USES[w]
                dst = bank_of(w)
                pe.wait_ge(*emptied(it, w - 2))
                if u[0] == "lnT":
                    i = NORMS.index(u[1])
                    pe.wait_ge(x_hat_made, nth(it, len(NORMS), i))
                    for k, (col, rows) in enumerate(widths(u[1][0])):
                        for tt in range(TT):
                            last = nc.tensor.transpose(dst[0:rows, k * N + tt * P:k * N + (tt + 1) * P],
                                                       x_hat[:, tt, col:col + rows], ident[:])
                elif u[0] == "chunk":
                    _, n, x, tt, half = u
                    kind = PASSES[n][0]
                    side = "ctx" if kind == "cross" and x != "q" else "ln"
                    weights = w_q[kind] if x == "q" else w_kv[kind]
                    col = half * CHUNK + (MID if x == "v" else 0)
                    if (x, tt, half) in (("q", 0, 0), ("k", 0, 0)):
                        pe.wait_ge(w_split, SPLIT[x, kind])
                        pe.wait_ge(a_T_ready, nth(it, len(NORMS), NORMS.index((side, n))))
                    for k, (_, rows) in enumerate(widths(side)):
                        last = product(dst[:], [a[0:rows, k, tt * P:(tt + 1) * P] for a in (c_T if side == "ctx" else a_T)],
                                       [m[0:rows, k, col:col + CHUNK] for m in weights], k == 0, k == KT - 1)
                elif u[0] == "turn":
                    _, n, x, tt, half = u
                    c = chunk_no(u)
                    pe.wait_ge(roped_low, nth(it, QK_CHUNKS, c))
                    first, heads = (2 * CHUNK, CH_HEADS // 2) if x == "q_low" else (0, CH_HEADS)
                    for h in range(heads):
                        last = nc.tensor.transpose(dst[:].bitcast(F16)[:, h * P:(h + 1) * P],
                                                   roped_parts[c % 2][:, first + h * P:first + (h + 1) * P], ident_16[:])
                elif u[0] == "wo":
                    n = u[1]
                    kind = PASSES[n][0]
                    pe.wait_ge(w_split, SPLIT["wo", kind])
                    pe.wait_ge(o_T_ready, nth(it, QUADS, 4 * n + 3))
                    for tt in range(TT):
                        for m in range(MT):
                            last = product(dst[:, tt * D:(tt + 1) * D], [o[:, m, tt * P:(tt + 1) * P] for o in o_T],
                                           [a[:, m, :] for a in w_o[kind]], m == 0, m == MT - 1)
                elif u[0] == "hidden":
                    _, s, j = u
                    if j == 0:
                        pe.wait_ge(w_split, SPLIT["ff_w1"])
                        pe.wait_ge(a_T_ready, nth(it, len(NORMS), NORMS.index(("ff", s))))
                    for i in range(2):
                        for k in range(KT):
                            last = product(dst[:, i * N:(i + 1) * N],
                                           [a[:, k, (2 * j + i) * P:(2 * j + i + 1) * P] for a in w_1],
                                           [a[:, k, :] for a in a_T], k == 0, k == KT - 1)
                else:
                    s = u[1]
                    pe.wait_ge(w_split, SPLIT["ff_w2"])
                    pe.wait_ge(hidden_ready, nth(it, len(HIDDENS), (s + 1) * (len(HIDDENS) // 2) - 1))
                    for tt in range(TT):
                        for m in range(FF // P):
                            last = product(dst[:, tt * D:(tt + 1) * D], [a[:, m, tt * P:(tt + 1) * P] for a in h_T],
                                           [a[:, m, :] for a in w_2], m == 0, m == FF // P - 1)
                return last

            with pe.Fori(0, ITERS) as it:
                for kind, x in SCHEDULE:
                    if kind == "bank":
                        fill_bank(it, BANK_USES.index(x)).then_inc(bank_filled, 1)
                    elif kind == "step":
                        n, step = x
                        if step < H:
                            h = n * H + step
                            if step == 0:
                                pe.wait_ge(q_T_ready, nth(it, len(Q_TURNS), (n + 1) * (len(Q_TURNS) // 4) - 1))
                                pe.wait_ge(k_T_ready, nth(it, len(K_TURNS), (n + 1) * (len(K_TURNS) // 4) - 1))
                            pe.wait_ge(probs_made, nth(it, HEADS, h - 2))
                            for tt in range(TT):
                                dst, keys = ps_scores[h % 2][:, tt * N:(tt + 1) * N], turned_parts["k"][n % 2]
                                nc.tensor.matmul(dst, turned_parts["q"][n % 2][:, step, tt * P:(tt + 1) * P],
                                                 keys[:, step, :], start=True, stop=False)
                                lo = DH * (step % 2)
                                last = nc.tensor.matmul(
                                    dst, turned_parts["q_low"][n % 2][lo:lo + DH, step // 2, tt * P:(tt + 1) * P],
                                    keys[lo:lo + DH, step, :], start=False, stop=True)
                            last.then_inc(scores_made, 1)
                        if TURN_LAG <= step < H + TURN_LAG:
                            h = n * H + step - TURN_LAG
                            pe.wait_ge(probs_scaled, nth(it, HEADS, h))
                            pe.wait_ge(probs_T_ready, nth(it, HEADS, h - 2))
                            for tt in range(TT):
                                for m in range(TT):
                                    last = nc.tensor.transpose(
                                        ps_probs_T[h % 2][:, m * N + tt * P:m * N + (tt + 1) * P],
                                        probs[h % NP][:, tt, m * P:(m + 1) * P], ident[:])
                            last.then_inc(probs_turned, 1)
                        if PV_LAG <= step:
                            head = step - PV_LAG
                            h = n * H + head
                            if head == 0:
                                pe.wait_ge(v_ready, nth(it, QK_CHUNKS // 2, (n + 1) * (QK_CHUNKS // 8) - 1))
                            pe.wait_ge(probs_T_ready, nth(it, HEADS, h))
                            quad = h // 4
                            if head % 4 == 0:
                                pe.wait_ge(o_T_ready, nth(it, QUADS, quad - 2))
                            lo, col = DH * (head % 2), N * (head // 2 % 2)
                            for m in range(TT):
                                last = nc.tensor.matmul(ps_o[quad % 2][lo:lo + DH, col:col + N],
                                                        v[n % 2][:, m, head * DH:(head + 1) * DH],
                                                        probs_T[h % 2][:, m, :], start=(m == 0), stop=(m == TT - 1))
                            last.then_inc(pv_made, 1)


INPUTS = ["x", "cond_1024", "ctx_768"] + [f"L0_xcond_{x}" for x in (
    "ln1_w", "ln1_b", "g1_w", "g1_b", "b1_w", "b1_b", "ln2_w", "ln2_b", "g2_w", "g2_b", "b2_w", "b2_b", "sa_wq",
    "sa_wkv", "sa_wo", "sa_bo", "ca_lnc_w", "ca_lnc_b", "ca_wq", "ca_wkv", "ca_wo", "ca_bo", "ff_w1", "ff_b1",
    "ff_w2", "ff_b2")]


def kernel(**inputs):
    import numpy as np
    import concourse.bacc as bacc
    from concourse.bass_utils import run_bass_kernel_spmd

    inv = (1.0 / 10000.0 ** (np.arange(0, DH, 2, dtype=np.float32) / DH)).astype(np.float32)
    angle = np.arange(N, dtype=np.float32)[:, None] * inv[None, :]
    cos = np.cos(angle)
    sin = np.stack((-np.sin(angle), np.sin(angle)), axis=-1).reshape(N, DH)
    scale = np.float32(DH ** -0.5)
    cos, sin = cos / np.float32(W_SCALE), sin / np.float32(W_SCALE)
    arrays = {"rope_cos_q": cos * scale, "rope_sin_q": sin * scale, "rope_cos_k": cos, "rope_sin_k": sin}
    arrays = {k: np.ascontiguousarray(a.astype(np.float32)) for k, a in arrays.items()}
    for name in INPUTS:
        arrays[name] = np.ascontiguousarray(inputs[name])

    nc = bacc.Bacc("TRN2", target_bir_lowering=False, num_devices=1)
    t = {k: nc.dram_tensor(f"in_{k}", a.shape, mybir.dt.from_np(a.dtype), kind="ExternalInput").ap()
         for k, a in arrays.items()}
    t["out"] = nc.dram_tensor("out_0", (BATCH, N, D), F32, kind="ExternalOutput").ap()
    block_kernel(nc, t)
    r = run_bass_kernel_spmd(nc, [{f"in_{k}": a for k, a in arrays.items()}], core_ids=[0])
    return r.results[0]["out_0"]
```

```python
from contextlib import ExitStack

import concourse.bass as bass
from concourse import mybir

F32 = mybir.dt.float32
F16 = mybir.dt.float16
ALU = mybir.AluOpType
ACT = mybir.ActivationFunctionType
AX = mybir.AxisListType

P = 128
BATCH, N, D = 16, 256, 256
H, DH = 16, 64
MID = H * DH
DC = 192
FF = 4 * D
EPS = 1e-5
TT = N // P
KT = D // P
CHUNK = 512
HALVES = MID // CHUNK
CH_HEADS = CHUNK // DH
PAIRS = H // 2
MT = MID // P
FF_HALF = FF // P // 2
SLOTS = 2
BANKS = 3
ITERS = BATCH // SLOTS
TURN_LAG = 3
PV_LAG = 3
W_SCALE = 64.0

PASSES = [("self", 0), ("self", 1), ("cross", 0), ("cross", 1)]

HID0 = 8
HID1 = 12
LN_STEP = (2, 13, 13, 13)
OUT_LAG = 2
LN_LAG = 1
LOW_LAG = 1
TURN_STEPS = 3
CROSS_K = (0, 1, 3, 4)
CROSS_V = (5, 7, 10, 13)
CROSS_Q = (8, 9, 11, 12)
SELF_Q = (0, 3, 6, 9)
SELF_K = (1, 4, 7, 10)
SELF_V = (5, 8, 11, 13)


def order(item):
    kind, x = item
    if kind == "bank":
        kind = x[0]
    return ORDER.index(kind) if kind in ORDER else len(ORDER)


ORDER = ["stats", "norm", "chunk"]


def make_schedule():
    after = {(n, step): [] for n in range(len(PASSES)) for step in range(H)}

    def put(n, step, *items):
        after[n, step] += items

    def chunk(n, step, x, tt, half):
        c = ("chunk", (n + 1) % len(PASSES), x, tt, half)
        put(n, step, ("bank", c))
        if x != "v":
            put(n, step + 1, ("high", c))
            put(n, step + LOW_LAG, ("low", c))
            for part in (["q", "q_low"] if x == "q" else ["k"]):
                put(n, min(step + TURN_STEPS, H - 1), ("bank", ("turn", c[1], part, tt, half)))

    def layernorm(n, step, x):
        put(n, step, ("stats", x))
        put(n, step + 1, ("norm", x))
        put(n, step + 2, ("bank", ("lnT", x)))

    every = [(tt, half) for tt in range(TT) for half in range(HALVES)]
    for n in range(len(PASSES)):
        for half in range(2):
            put(n, (WO_FIRST, WO_STEP)[half], ("bank", ("wo", (n - 1) % len(PASSES), half)))
        if n in (1, 2):
            layernorm(n, WO_STEP + LN_LAG, ("ln", n + 1))
            for i, part in enumerate(every):
                chunk(n, CROSS_K[i], "k", *part)
                chunk(n, CROSS_V[i], "v", *part)
                chunk(n, CROSS_Q[i], "q", *part)
        else:
            slot = 1 if n == 0 else 0
            layernorm(n, WO_STEP + LN_LAG, ("ff", slot))
            for i, part in enumerate(every):
                chunk(n, SELF_Q[i], "q", *part)
                chunk(n, SELF_K[i], "k", *part)
                chunk(n, SELF_V[i], "v", *part)
            for half in range(2):
                put(n, (HID0, HID1)[half] + OUT_LAG, ("bank", ("out", slot, half)))
            for j in range(FF // P // 2):
                step = (HID0, HID0, HID1, HID1)[j]
                put(n, step, ("bank", ("hidden", slot, j)))
                put(n, step + 1, ("hidden low", (slot, j)))
            put(n, 15, ("store", slot))
        layernorm(n, LN_STEP[n], (("ctx", 2), ("ctx", 3), ("ln", 0), ("ln", 1))[n])
    s = []
    for n, step in after:
        items = sorted(after[n, step], key=order)
        s += [("step", (n, step))] + items + [("pv", (n, step))]
    return s


def offset(kind, x):
    if kind == "bank" and x[0] == "lnT":
        kind, x = "norm", x[1]
    if kind in ("stats", "norm"):
        return {("ln", 0): 1, ("ln", 1): 1, ("ff", 1): -1}.get(x, 0)
    if kind in ("high", "low") or kind == "bank" and x[0] in ("chunk", "turn"):
        return 1 if x[1] == 0 else 0
    if kind == "hidden low":
        return -x[0]
    if kind == "store" or kind == "bank" and x[0] in ("hidden", "out"):
        return -1 if x == 1 or kind == "bank" and x[1] == 1 else 0
    if kind == "bank" and x[:2] == ("wo", 3):
        return -1
    return 0


def exists(it):
    return not isinstance(it, int) or 0 <= it < ITERS


WO_FIRST = 2
WO_STEP = PV_LAG + 1
SCHEDULE = make_schedule()
LAST_PART = max(i for i, item in enumerate(SCHEDULE) if offset(*item) == -1) + 1
BANK_USES = [x for kind, x in SCHEDULE if kind == "bank"]
NORMS = [x for kind, x in SCHEDULE if kind == "stats"]
BIASED = [x for x in NORMS if x[0] != "ctx"]
BANK_OF = [w % BANKS for w in range(len(BANK_USES))]
if len(BANK_USES) % BANKS == 1:
    BANK_OF[-1] = 1
assert len(NORMS) % 2 == 0
RESIDUALS = [(kind, n, half) for kind, n in (("wo", 0), ("wo", 1), ("wo", 2), ("out", 0), ("wo", 3), ("out", 1))
             for half in range(2)]
USES = sorted(BANK_USES, key=lambda x: x[1] if isinstance(x[1], int) else 0)
QK = [x for x in USES if x[0] == "chunk" and x[2] != "v"]
TURNS = {part: [x for x in USES if x[0] == "turn" and x[2] == part] for part in ("q", "q_low", "k")}
V_CHUNKS = [x for x in USES if x[0] == "chunk" and x[2] == "v"]
HIDDENS = [x for x in USES if x[0] == "hidden"]

VECTOR_LOADS = 3 + 10 * KT + 1


def vector_loads(t, bias_row, vec, ff_b1):
    for x, name in (("self", "sa_bo"), ("cross", "ca_bo"), ("ff", "ff_b2")):
        yield bias_row[x][:], t[f"L0_xcond_{name}"].unsqueeze(0).broadcast_to([P, D])
    for x, dst in vec.items():
        src = t[f"L0_xcond_{x}"].unsqueeze(1)
        for k, (col, rows) in enumerate([(0, P), (P, DC - P if x.startswith("ca") else P)]):
            yield dst[0:rows, k:k + 1], src[col:col + rows, :]
    yield ff_b1[:], t["L0_xcond_ff_b1"].rearrange("(t p) -> p t", p=P)


def block_kernel(nc, t):
    with ExitStack() as ctx:
        def sb(name, shape, dt=F32):
            return ctx.enter_context(nc.sbuf_tensor(name, shape, dt))

        def pb(name):
            return ctx.enter_context(nc.psum_tensor(name, [P, 512], F32))

        def sem(name):
            return ctx.enter_context(nc.semaphore(name))

        def parts(name, shape):
            return [sb(f"{name}_{part}", shape, F16) for part in ("high", "low")]

        w_q = {"self": parts("w_sa_q", [P, KT, MID]), "cross": parts("w_ca_q", [P, KT, MID])}
        w_kv = {"self": parts("w_sa_kv", [P, KT, 2 * MID]), "cross": parts("w_ca_kv", [P, KT, 2 * MID])}
        w_o = {"self": parts("w_sa_o", [P, MT, D]), "cross": parts("w_ca_o", [P, MT, D])}
        w_1 = parts("w_1", [P, KT, FF])
        w_2 = parts("w_2", [P, FF // P, D])
        bias_row = {x: sb(f"bias_{x}", [P, D]) for x in ("self", "cross", "ff")}
        vec = {x: sb(f"vec_{x}", [P, KT]) for x in (
            "ln1_w", "ln1_b", "g1_b", "b1_b", "ln2_w", "ln2_b", "g2_b", "b2_b", "ca_lnc_w", "ca_lnc_b")}
        ff_b1 = sb("ff_b1", [P, FF // P])
        rope_cos = {x: sb(f"rope_cos_{x}", [P, TT, DH // 2]) for x in "qk"}
        rope_sin = {x: sb(f"rope_sin_{x}", [P, TT, DH]) for x in "qk"}
        ident = sb("ident", [P, P])
        ident_16 = sb("ident_16", [P, P], F16)
        minus_half = sb("minus_half", [P, TT])
        gain = {x: sb(f"gain_{x}", [P, KT, BATCH]) for x in ("1", "2")}
        shift = {x: sb(f"shift_{x}", [P, KT, BATCH]) for x in ("1", "2")}

        x_in = [sb(f"x_in{s}", [P, TT, D]) for s in range(SLOTS)]
        c_in = [sb(f"c_in{s}", [P, TT, DC]) for s in range(SLOTS)]
        x_res = [sb(f"x_res{s}", [P, TT, D]) for s in range(SLOTS)]
        stats = [sb(f"stats{i}", [P, TT, 6]) for i in range(2)]
        moments = [sb(f"moments{i}", [P, TT, 2]) for i in range(2)]
        var_eps = [sb(f"var_eps{i}", [P, TT]) for i in range(2)]
        rstd = [sb(f"rstd{i}", [P, TT]) for i in range(2)]
        x_hat = sb("x_hat", [P, TT, D])
        y_T = sb("y_T", [P, KT, N])
        a_T = {x: parts(f"{x}_T", [P, KT, N]) for x in ("ln", "ctx", "ff")}
        x_cos = [sb(f"x_cos{i}", [P, CHUNK]) for i in range(2)]
        x_sin = [sb(f"x_sin{i}", [P, CHUNK]) for i in range(2)]
        roped = x_cos
        roped_parts = [sb(f"roped_parts{i}", [P, 3 * CHUNK], F16) for i in range(2)]
        turned_parts = {x: [sb(f"{x}_T{i}", [P, heads, N], F16) for i in range(2)]
                        for x, heads in (("q", H), ("k", H), ("q_low", PAIRS))}
        o_parts = sb("o_parts", [P, 2, PAIRS, N], F16)
        o_T = [o_parts[:, i] for i in range(2)]
        gelu = sb("gelu", [P, 2, CHUNK])
        h_parts = sb("h_parts", [P, 2, FF_HALF, N], F16)
        h_T = [h_parts[:, i] for i in range(2)]
        w_cond = {x: turned_parts["q"][1][:].rearrange("p a n -> p (a n)").bitcast(F32)[
            :, i * KT * D:(i + 1) * KT * D].rearrange("p (t n) -> p t n", t=KT)
            for i, x in enumerate(("g1", "b1", "g2", "b2"))}
        v = [sb(f"v{i}", [P, TT, MID]) for i in range(2)]
        NP = 4
        staging = [v[1][:].rearrange("p t n -> p (t n)"),
                   turned_parts["k"][1][:].rearrange("p a n -> p (a n)").bitcast(F32),
                   o_parts[:].rearrange("p i a n -> p (i a n)").bitcast(F32)]
        probs = [sb(f"probs{i}", [P, TT, N]) for i in range(NP)]
        cond = probs[0][0:BATCH, 0, :]
        cond_T = probs[1][:, 0, 0:KT * BATCH].rearrange("p (t b) -> p t b", t=KT)
        one_plus_g = probs[2][:, 0, 0:2 * KT * BATCH].rearrange("p (i t b) -> p i t b", i=2, t=KT)
        probs_T = [sb(f"probs_T{i}", [P, TT, N]) for i in range(2)]
        neg_max = sb("neg_max", [P, NP, TT])
        row_sum = sb("row_sum", [P, NP, TT])
        row_inv = sb("row_inv", [P, NP, TT])

        def slab(name, hl, k=None, first=0, rows=P, copies=1):
            src = t[f"L0_xcond_{name}"]
            if k is not None:
                return src[first:first + rows, :], [w[0:rows * copies, k, :] for w in hl], rows, copies
            return src.rearrange("(t p) n -> p t n", p=P), [w[:].rearrange("p t n -> p (t n)") for w in hl], rows, 1

        SLABS = [slab("sa_wq", w_q["self"]), slab("sa_wkv", w_kv["self"], 0, 0), slab("sa_wkv", w_kv["self"], 1, P),
                 slab("sa_wo", w_o["self"]), slab("ca_wq", w_q["cross"]), slab("ca_wkv", w_kv["cross"], 0, 0),
                 slab("ca_wkv", w_kv["cross"], 1, P, DC - P, 2), slab("ca_wo", w_o["cross"]), slab("ff_w1", w_1),
                 slab("ff_w2", w_2)]
        FIRST_SLABS = 3
        SPLIT = {("q", "self"): 1, ("k", "self"): 3, ("wo", "self"): 4, ("q", "cross"): 5, ("k", "cross"): 7,
                 ("wo", "cross"): 8, "ff_w1": 9, "ff_w2": 10}

        bank = [pb(f"bank{i}") for i in range(BANKS)]
        ps_scores = [pb("ps_scores0"), pb("ps_scores1")]
        ps_probs_T = pb("ps_probs_T")
        ps_o = [pb("ps_o0"), pb("ps_o1")]

        vectors_loaded, rope_loaded, cond_loaded = sem("vectors_loaded"), sem("rope_loaded"), sem("cond_loaded")
        slab_loaded = [sem(f"slab_loaded{i}") for i in range(len(staging))]
        w_high_made, w_split = sem("w_high_made"), sem("w_split")
        x_loaded = [sem(f"x_loaded{s}") for s in range(SLOTS)]
        c_loaded = [sem(f"c_loaded{s}") for s in range(SLOTS)]
        stored = [sem(f"stored{s}") for s in range(SLOTS)]
        ident_made = sem("ident_made")
        cond_turned, cond_copied, cond_projected, cond_ready = (
            sem("cond_turned"), sem("cond_copied"), sem("cond_projected"), sem("cond_ready"))
        bank_filled = sem("bank_filled")
        stats_made, moments_made, var_made, rstd_made, x_hat_made = (
            sem("stats_made"), sem("moments_made"), sem("var_made"), sem("rstd_made"), sem("x_hat_made"))
        a_T_ready = sem("a_T_ready")
        biased_made, residual_made = sem("biased_made"), sem("residual_made")
        y_T_made, a_high_made = sem("y_T_made"), sem("a_high_made")
        parts_made, roped_made, roped_high, roped_low = (
            sem("parts_made"), sem("roped_made"), sem("roped_high"), sem("roped_low"))
        q_T_ready, q_low_T_ready, k_T_ready, v_ready = (
            sem("q_T_ready"), sem("q_low_T_ready"), sem("k_T_ready"), sem("v_ready"))
        turn_ready = {"q": q_T_ready, "q_low": q_low_T_ready, "k": k_T_ready}
        scores_made, max_made, probs_made, inv_made, probs_scaled = (
            sem("scores_made"), sem("max_made"), sem("probs_made"), sem("inv_made"), sem("probs_scaled"))
        probs_turned, probs_T_ready, pv_made, o_T_ready = (
            sem("probs_turned"), sem("probs_T_ready"), sem("pv_made"), sem("o_T_ready"))
        o_high_made, gelu_made, hidden_high, hidden_ready = (
            sem("o_high_made"), sem("gelu_made"), sem("hidden_high"), sem("hidden_ready"))
        sp_passed, dve_passed = sem("sp_passed"), sem("dve_passed")

        CREDIT = 96
        credited = [*x_loaded, *c_loaded, *stored, bank_filled, stats_made, moments_made, var_made, rstd_made,
                    x_hat_made, y_T_made, a_high_made, a_T_ready, biased_made, residual_made, parts_made, roped_made,
                    roped_high, roped_low, q_T_ready, q_low_T_ready, k_T_ready, v_ready, scores_made, max_made, probs_made, inv_made,
                    probs_scaled, probs_turned, probs_T_ready, pv_made, o_high_made, o_T_ready, gelu_made,
                    hidden_high, hidden_ready]

        def nth(it, per_iteration, ordinal):
            return it * per_iteration + (ordinal + 1 + CREDIT)

        def nth_in_bodies(b, per_body, ordinal):
            return b * per_body + (per_body + ordinal + 1 + CREDIT)

        def filled(b, w):
            return nth_in_bodies(b, len(BANK_USES), w)

        def normed(it, x):
            return nth_in_bodies(it - offset("norm", x), len(NORMS), NORMS.index(x))

        def nth_dma(it):
            return it * 16 + (16 + CREDIT)

        def chunk_no(u):
            _, n, x, tt, half = u
            return QK.index(("chunk", n, x[0], tt, half))

        LAST_TURNS = sorted([x for x in BANK_USES if x[0] == "turn" and x[2] != "q"], key=chunk_no)
        HEADS = len(PASSES) * H
        QUADS = HEADS // 4

        def back(it, h):
            return (it, h) if h >= 0 else (it - 1, h + HEADS)

        def stand_in(engine, semaphore, count):
            engine.wait_ge(semaphore, count - 1)
            engine.sem_inc(semaphore, 1)

        def bank_of(w):
            return bank[BANK_OF[w]]

        def turned(it, i):
            if i < 0:
                it, i = it - 1, i + len(LAST_TURNS)
            u = LAST_TURNS[i]
            return filled(it - offset("bank", u), BANK_USES.index(u))

        def emptied_for(b, w):
            last = [i for i in range(len(BANK_USES)) if BANK_OF[i] == BANK_OF[w] and i != w]
            if last[0] > w:
                b, w = b - 1, last[-1]
            else:
                w = max(i for i in last if i < w)
            if isinstance(b, int) and b < -1:
                return None
            it = b + offset("bank", BANK_USES[w])
            if not exists(it):
                return emptied_for(b, w)
            u = BANK_USES[w]
            if u[0] == "lnT":
                return y_T_made, normed(it, u[1])
            if u[0] == "turn":
                return turn_ready[u[2]], nth(it, len(TURNS[u[2]]), TURNS[u[2]].index(u))
            if u[0] == "hidden":
                return gelu_made, nth(it, len(HIDDENS), HIDDENS.index(u))
            if u[0] in ("wo", "out"):
                return residual_made, nth(it, len(RESIDUALS), RESIDUALS.index(u))
            if u[2] == "v":
                return v_ready, nth(it, len(V_CHUNKS), V_CHUNKS.index(u))
            return parts_made, nth(it, len(QK), chunk_no(u))

        def high_of(x, c):
            if x == "q":
                return roped_parts[c % 2][:, 0:2 * CHUNK].rearrange("p (a two c d) -> p a two c d", two=2, c=2, d=DH)
            return roped_parts[c % 2][:, 0:2 * CHUNK].rearrange("p (a four c d) -> p a four c d", four=4, c=1, d=DH)[
                :, :, 0:4:3]

        def low_of(x, c):
            if x == "q":
                return roped_parts[c % 2][:, 2 * CHUNK:3 * CHUNK].rearrange("p (a two d) -> p a two d", two=2, d=DH)
            return roped_parts[c % 2][:, 0:2 * CHUNK].rearrange("p (a four d) -> p a four d", four=4, d=DH)[:, :, 1:3]

        def source(x):
            kind, n = x
            if kind == "ctx":
                return c_in[PASSES[n][1]]
            if kind == "ff":
                return x_res[n]
            return x_in[n] if n < 2 else x_res[n - 2]

        def stream(u):
            kind, n, half = u
            slot = n % 2
            return (x_in if kind == "wo" and n < 2 and half == 0 else x_res)[slot], x_res[slot]

        def widths(kind):
            return [(0, P), (P, DC - P)] if kind == "ctx" else [(0, P), (P, P)]

        block = ctx.enter_context(nc.Block())

        @block.sync
        def _(sp):
            def load(dst, src, s):
                sp.dma_start(dst, src).then_inc(s, 16)

            def load_x(b, s):
                sp.dma_start(x_in[s][:], t["x"][bass.ds(b, 1), :, :].rearrange(
                    "b (t p) d -> p (b t) d", p=P)).then_inc(x_loaded[s], 16)

            def load_c(b, s):
                sp.dma_start(c_in[s][:], t["ctx_768"][bass.ds(b, 1), :, :].rearrange(
                    "b (t p) d -> p (b t) d", p=P)).then_inc(c_loaded[s], 16)

            load_x(0, 0)
            load(cond, t["cond_1024"], cond_loaded)
            for x in ("g1", "b1", "g2", "b2"):
                load(w_cond[x], t[f"L0_xcond_{x}_w"].rearrange("(t p) n -> p t n", p=P), cond_loaded)
            for i, (src, _, rows, copies) in enumerate(SLABS):
                j = i % len(staging)
                if i >= len(staging):
                    sp.wait_ge(w_split, i - len(staging) + 1)
                for c in range(copies):
                    dst = staging[j][c * rows:(c + 1) * rows, :]
                    if len(src.shape) == 3:
                        dst = dst.rearrange("p (t n) -> p t n", t=src.shape[1])
                    load(dst, src, slab_loaded[j])
                if i == 2:
                    load_x(1, 1)
                    load_c(0, 0)
                    load_c(1, 1)
            with sp.Fori(1, ITERS) as it:
                for s in range(SLOTS):
                    sp.wait_ge(residual_made, nth(it - 1, len(RESIDUALS), RESIDUALS.index(("wo", s, 0))))
                    sp.sem_inc(sp_passed, 1)
                    load_x(it * SLOTS + s, s)
                for s in range(SLOTS):
                    sp.wait_ge(x_hat_made, normed(it - 1, ("ctx", 2 + s)))
                    sp.sem_inc(sp_passed, 1)
                    load_c(it * SLOTS + s, s)

        @block.gpsimd
        def _(pool):
            for s in credited:
                pool.sem_inc(s, CREDIT)
            nc.gpsimd.memset(minus_half[:], -0.5)
            nc.gpsimd.memset(ident[:], 0.0).then_inc(ident_made, 1)
            pool.wait_ge(ident_made, 1)
            nc.gpsimd.affine_select(out=ident[:], in_=ident[:], compare_op=ALU.not_equal, fill=1.0, base=0,
                                    pattern=[[-1, P]], channel_multiplier=1).then_inc(ident_made, 1)
            pool.wait_ge(ident_made, 2)
            nc.gpsimd.tensor_copy(ident_16[:], ident[:]).then_inc(ident_made, 1)
            pool.wait_ge(vectors_loaded, 16 * VECTOR_LOADS)

            def add_bias(it, x):
                kind, n = x
                src = stream(("out" if kind == "ff" else "wo", n, 0))[0]
                pool.wait_ge(x_hat_made, normed(it, x))
                row = bias_row["ff" if kind == "ff" else PASSES[n][0]]
                nc.gpsimd.tensor_tensor(out=src[:], in0=src[:], in1=row[:].unsqueeze(1).broadcast_to([P, TT, D]),
                                        op=ALU.add).then_inc(biased_made, 1)

            def body(b, items):
                for kind, x in items:
                    it = b + offset(kind, x)
                    if not exists(it):
                        if kind == "stats":
                            stand_in(pool, rstd_made, normed(it, x))
                            if x in BIASED:
                                stand_in(pool, biased_made, nth_in_bodies(b, len(BIASED), BIASED.index(x)))
                        if kind != "step":
                            continue
                    if kind == "stats":
                        n = NORMS.index(x)
                        pool.wait_ge(var_made, normed(it, x))
                        nc.gpsimd.tensor_tensor(out=rstd[n % 2][:], in0=var_eps[n % 2][:], in1=minus_half[:],
                                                op=ALU.pow).then_inc(rstd_made, 1)
                    elif kind == "bank" and x[0] == "chunk" and x[2] != "v":
                        c = chunk_no(x)
                        pool.wait_ge(parts_made, nth(it, len(QK), c))
                        nc.gpsimd.tensor_tensor(out=roped[c % 2][:], in0=x_cos[c % 2][:], in1=x_sin[c % 2][:],
                                                op=ALU.add).then_inc(roped_made, 1)
                    elif kind == "low":
                        c = chunk_no(x)
                        pool.wait_ge(roped_high, nth(it, len(QK), c))
                        nc.gpsimd.tensor_tensor(out=low_of(x[2], c),
                                                in0=roped[c % 2][:].rearrange("p (a two d) -> p a two d", two=2, d=DH),
                                                in1=high_of(x[2], c)[:, :, :, 0, :], op=ALU.subtract).then_inc(roped_low, 1)
                    elif kind == "bank" and x[0] == "lnT" and x[1][0] != "ctx":
                        add_bias(it, x[1])
                    elif kind == "step":
                        n, step = x
                        ith, h = back(it, n * H + step - 1)
                        if exists(ith):
                            pool.wait_ge(inv_made, nth(ith, HEADS, h))
                            nc.gpsimd.tensor_tensor(
                                out=probs[h % NP][:], in0=probs[h % NP][:],
                                in1=row_inv[:, h % NP, :].unsqueeze(2).broadcast_to([P, TT, N]),
                                op=ALU.mult).then_inc(probs_scaled, 1)

            body(-1, SCHEDULE)
            body(0, SCHEDULE)
            with pool.Fori(1, ITERS - 1) as b:
                body(b, SCHEDULE)
            body(ITERS - 1, SCHEDULE)
            body(ITERS, SCHEDULE[:LAST_PART])

        @block.vector
        def _(dve):
            def condition():
                dve.wait_ge(cond_turned, 1)
                nc.vector.tensor_copy(cond_T, bank[0][:, 0:KT * BATCH].rearrange(
                    "p (t b) -> p t b", t=KT)).then_inc(cond_copied, 1)
                dve.wait_ge(vectors_loaded, 16 * VECTOR_LOADS)
                dve.wait_ge(cond_projected, 1)
                made = bank[1][:, 0:4 * KT * BATCH].rearrange("p (m t b) -> p m t b", m=4, t=KT)
                for i, x in enumerate("12"):
                    for k in range(KT):
                        nc.vector.tensor_scalar(one_plus_g[:, i, k, :], made[:, 2 * i, k, :], vec[f"g{x}_b"][:, k:k + 1],
                                                1.0, ALU.add, ALU.add)
                        last = nc.vector.tensor_scalar(shift[x][:, k, :], made[:, 2 * i + 1, k, :],
                                                       vec[f"b{x}_b"][:, k:k + 1], None, ALU.add)
                last.then_inc(cond_ready, 1)
                dve.wait_ge(cond_ready, 1)
                for i, x in enumerate("12"):
                    for k in range(KT):
                        nc.vector.tensor_scalar(gain[x][:, k, :], one_plus_g[:, i, k, :], vec[f"ln{x}_w"][:, k:k + 1],
                                                None, ALU.mult)
                        last = nc.vector.scalar_tensor_tensor(
                            out=shift[x][:, k, :], in0=one_plus_g[:, i, k, :], scalar=vec[f"ln{x}_b"][:, k:k + 1],
                            in1=shift[x][:, k, :], op0=ALU.mult, op1=ALU.add)
                last.then_inc(cond_ready, 1)

            def split(i):
                _, (high, low), rows, copies = SLABS[i]
                dve.wait_ge(w_high_made, i + 1)
                nc.vector.scalar_tensor_tensor(out=low, in0=staging[i % len(staging)][0:rows * copies, :], scalar=W_SCALE,
                                               in1=high, op0=ALU.mult, op1=ALU.subtract).then_inc(w_split, 1)

            condition()
            dve.wait_ge(rope_loaded, 16 * 4)
            dve.wait_ge(cond_ready, 2)

            def layernorm_stats(it, n):
                kind, at = NORMS[n]
                src, j = source(NORMS[n]), n % 2
                count = normed(it, NORMS[n])
                if kind == "ctx":
                    dve.wait_ge(c_loaded[PASSES[at][1]], nth_dma(it))
                elif kind == "ln" and at < 2:
                    dve.wait_ge(x_loaded[at], nth_dma(it))
                else:
                    r = RESIDUALS.index(("wo", at - 2 if kind == "ln" else at + 2, 1))
                    dve.wait_ge(residual_made, nth(it, len(RESIDUALS), r))
                dve.wait_ge(x_hat_made, count - 2)
                for tt in range(TT):
                    last = nc.vector.bn_stats(out=stats[j][:, tt, :], in_=src[:, tt, :])
                last.then_inc(stats_made, 1)
                dve.wait_ge(stats_made, count)
                dve.sem_inc(dve_passed, 1)
                for tt in range(TT):
                    last = nc.vector.bn_aggr(out=moments[j][:, tt, :], in_=stats[j][:, tt, :])
                last.then_inc(moments_made, 1)
                dve.wait_ge(moments_made, count)
                nc.vector.tensor_scalar(var_eps[j][:], moments[j][:, :, 1], EPS, None, ALU.add).then_inc(var_made, 1)

            def layernorm_apply(it, n):
                src, j = source(NORMS[n]), n % 2
                width = DC if NORMS[n][0] == "ctx" else D
                dve.wait_ge(rstd_made, normed(it, NORMS[n]))
                w = BANK_USES.index(("lnT", NORMS[n - 1]))
                dve.wait_ge(bank_filled, filled(it - offset("norm", NORMS[n]) - (0 if n else 1), w))
                for tt in range(TT):
                    last = nc.vector.tensor_scalar(x_hat[:, tt, 0:width], src[:, tt, :], moments[j][:, tt, 0:1],
                                                   rstd[j][:, tt:tt + 1], ALU.subtract, ALU.mult)
                last.then_inc(x_hat_made, 1)

            def empty_bank(b, it, w):
                u = BANK_USES[w]
                src = bank_of(w)
                if u[0] == "lnT":
                    kind, at = u[1]
                    dve.wait_ge(bank_filled, filled(b, w))
                    high, low = a_T[kind]
                    for k, (_, rows) in enumerate(widths(kind)):
                        if kind == "ctx":
                            g, b = vec["ca_lnc_w"][0:rows, k:k + 1], vec["ca_lnc_b"][0:rows, k:k + 1]
                        else:
                            which = "2" if kind == "ff" else "1"
                            s = at if kind == "ff" else PASSES[at][1]
                            g = gain[which][:, k, bass.ds(it * SLOTS + s, 1)]
                            b = shift[which][:, k, bass.ds(it * SLOTS + s, 1)]
                        last = nc.vector.tensor_scalar(y_T[0:rows, k, :], src[0:rows, k * N:(k + 1) * N], g, b,
                                                       ALU.mult, ALU.add)
                    last.then_inc(y_T_made, 1)
                    dve.wait_ge(y_T_made, normed(it, u[1]))
                    for k, (_, rows) in enumerate(widths(kind)):
                        last = nc.vector.tensor_copy(high[0:rows, k, :], y_T[0:rows, k, :])
                    last.then_inc(a_high_made, 1)
                    dve.wait_ge(a_high_made, normed(it, u[1]))
                    for k, (_, rows) in enumerate(widths(kind)):
                        dst = low[0:rows, k, :] if rows == P else high[rows:2 * rows, k, :]
                        last = nc.vector.tensor_tensor(out=dst, in0=y_T[0:rows, k, :],
                                                       in1=high[0:rows, k, :], op=ALU.subtract)
                    last.then_inc(a_T_ready, 1)
                elif u[0] == "turn" and u[2] == "q":
                    _, n, x, tt, half = u
                    dve.wait_ge(bank_filled, filled(b, w))
                    nc.vector.tensor_copy(
                        turned_parts["q"][n % 2][:, half * CH_HEADS:(half + 1) * CH_HEADS, tt * P:(tt + 1) * P],
                        src[:].bitcast(F16).rearrange("p (h n) -> p h n", h=CH_HEADS)).then_inc(q_T_ready, 1)
                elif u[0] == "chunk" and u[2] != "v":
                    _, n, x, tt, half = u
                    c = chunk_no(u)
                    dve.wait_ge(bank_filled, filled(b, w))
                    dve.wait_ge(roped_low, nth(it, len(QK), c - 2))
                    pairs = "p (h j two) -> p h j two"
                    cos = rope_cos[x][:, tt, :].unsqueeze(1).unsqueeze(3).broadcast_to([P, CH_HEADS, DH // 2, 2])
                    nc.vector.tensor_tensor(out=x_cos[c % 2][:].rearrange(pairs, two=2, j=DH // 2),
                                            in0=src[:].rearrange(pairs, two=2, j=DH // 2), in1=cos, op=ALU.mult)
                    sin = rope_sin[x][:, tt, :].rearrange("p (j two) -> p j two", two=2)
                    sin = sin.unsqueeze(1).broadcast_to([P, CH_HEADS, DH // 2, 2])
                    nc.vector.tensor_tensor(out=x_sin[c % 2][:].rearrange(pairs, two=2, j=DH // 2),
                                            in0=src[:].rearrange(pairs, two=2, j=DH // 2)[:, :, :, ::-1],
                                            in1=sin, op=ALU.mult).then_inc(parts_made, 1)
                elif u[0] in ("wo", "out"):
                    r = RESIDUALS.index(u)
                    dve.wait_ge(bank_filled, filled(b, w))
                    x = ("ff" if u[0] == "out" else "ln", u[1])
                    dve.wait_ge(biased_made, nth_in_bodies(it - offset("norm", x), len(BIASED), BIASED.index(x)))
                    if u[0] == "wo" and u[1] < 2 and u[2] == 0:
                        dve.wait_ge(stored[u[1]], nth_dma(it - 1))
                    before, after = stream(u)
                    flat = "p t d -> p (t d)"
                    nc.vector.scalar_tensor_tensor(out=after[:].rearrange(flat), in0=src[:], scalar=1.0 / W_SCALE,
                                                   in1=before[:].rearrange(flat), op0=ALU.mult,
                                                   op1=ALU.add).then_inc(residual_made, 1)

            def body(b, items):
                slabs = iter(range(FIRST_SLABS, len(SLABS)))
                for kind, x in items:
                    it = b + offset(kind, x)
                    if not exists(it):
                        if kind == "stats":
                            for made in (stats_made, moments_made, var_made, x_hat_made, y_T_made, a_high_made,
                                         a_T_ready):
                                stand_in(dve, made, normed(it, x))
                        if kind != "step":
                            continue
                    if kind == "stats":
                        layernorm_stats(it, NORMS.index(x))
                    elif kind == "norm":
                        layernorm_apply(it, NORMS.index(x))
                        if isinstance(b, int) and b == -1 and x == ("ln", 0):
                            for i in range(FIRST_SLABS):
                                split(i)
                    elif kind == "hidden low":
                        m = 2 * x[1] % FF_HALF
                        j = HIDDENS.index(("hidden", *x))
                        dve.wait_ge(hidden_high, nth(it, len(HIDDENS), j))
                        high, low = [h[:, m:m + 2, :].rearrange("p m n -> p (m n)") for h in h_T]
                        nc.vector.tensor_tensor(out=low, in0=gelu[:, j % 2], in1=high,
                                                op=ALU.subtract).then_inc(hidden_ready, 1)
                    elif kind == "bank":
                        empty_bank(b, it, BANK_USES.index(x))
                        if isinstance(b, int) and b == -1 and x[0] == "chunk" and (i := next(slabs, None)) is not None:
                            split(i)
                    elif kind == "step":
                        n, step = x
                        ith, h = back(it, n * H + step - TURN_LAG)
                        if exists(ith):
                            dve.wait_ge(probs_turned, nth(ith, HEADS, h))
                            dve.wait_ge(pv_made, nth(ith, HEADS, h - 2))
                            nc.vector.tensor_copy(probs_T[h % 2][:].rearrange("p t n -> p (t n)"),
                                                  ps_probs_T[:]).then_inc(probs_T_ready, 1)
                        h = n * H + step
                        if exists(it):
                            dve.wait_ge(scores_made, nth(it, HEADS, h))
                            nc.vector.tensor_reduce(
                                out=neg_max[:, h % NP, :], in_=ps_scores[h % 2][:].rearrange("p (t m) -> p t m", t=TT),
                                axis=AX.X, op=ALU.max, negate=True).then_inc(max_made, 1)
                        ith, h = back(it, n * H + step - 1)
                        if exists(ith):
                            dve.wait_ge(probs_made, nth(ith, HEADS, h))
                            nc.vector.reciprocal(row_inv[:, h % NP, :], row_sum[:, h % NP, :]).then_inc(inv_made, 1)
                        ith, h = back(it, n * H + step - PV_LAG - 2)
                        if exists(ith) and h % 4 == 3:
                            quad = h // 4
                            q = quad % 4
                            dve.wait_ge(o_high_made, nth(ith, QUADS, quad))
                            high, low = [o[:, 2 * q:2 * q + 2, :].rearrange("p a n -> p (a n)") for o in o_T]
                            nc.vector.tensor_tensor(out=low, in0=ps_o[quad % 2][:], in1=high,
                                                    op=ALU.subtract).then_inc(o_T_ready, 1)

            body(-1, SCHEDULE)
            body(0, SCHEDULE)
            with dve.Fori(1, ITERS - 1) as b:
                body(b, SCHEDULE)
            body(ITERS - 1, SCHEDULE)
            body(ITERS, SCHEDULE[:LAST_PART])

        @block.scalar
        def _(act):
            for dst, src in vector_loads(t, bias_row, vec, ff_b1):
                act.dma_start(dst, src, allow_slow_non_contiguous=True).then_inc(vectors_loaded, 16)
            for x in "qk":
                act.dma_start(rope_cos[x][:], t[f"rope_cos_{x}"].rearrange("(t p) d -> p t d", p=P)).then_inc(rope_loaded, 16)
                act.dma_start(rope_sin[x][:], t[f"rope_sin_{x}"].rearrange("(t p) d -> p t d", p=P)).then_inc(rope_loaded, 16)
            def split(i):
                _, (high, low), rows, copies = SLABS[i]
                act.wait_ge(slab_loaded[i % len(staging)],
                            16 * sum(SLABS[j][3] for j in range(i % len(staging), i + 1, len(staging))))
                nc.scalar.activation(high, staging[i % len(staging)][0:rows * copies, :], ACT.Copy,
                                     scale=W_SCALE).then_inc(w_high_made, 1)

            for i in range(FIRST_SLABS):
                split(i)

            def empty_bank(b, it, w):
                u = BANK_USES[w]
                src = bank_of(w)
                if u[0] == "turn" and u[2] != "q":
                    _, n, x, tt, half = u
                    heads = CH_HEADS // (2 if x == "q_low" else 1)
                    act.wait_ge(bank_filled, filled(b, w))
                    nc.scalar.activation(
                        turned_parts[x][n % 2][:, half * heads:(half + 1) * heads, tt * P:(tt + 1) * P],
                        src[:].bitcast(F16)[:, 0:heads * P].rearrange("p (h n) -> p h n", h=heads),
                        ACT.Copy).then_inc(turn_ready[x], 1)
                elif u[0] == "chunk" and u[2] == "v":
                    _, n, x, tt, half = u
                    act.wait_ge(bank_filled, filled(b, w))
                    nc.scalar.activation(v[n % 2][:, tt, half * CHUNK:(half + 1) * CHUNK], src[:],
                                         ACT.Copy, scale=1.0 / W_SCALE).then_inc(v_ready, 1)
                elif u[0] == "hidden":
                    j = HIDDENS.index(u)
                    m = 2 * u[2]
                    to = m % FF_HALF
                    act.wait_ge(bank_filled, filled(b, w))
                    act.wait_ge(hidden_ready, nth(it, len(HIDDENS), j - 2))
                    for i in range(2):
                        last = nc.scalar.activation(gelu[:, j % 2, i * N:(i + 1) * N], src[:, i * N:(i + 1) * N],
                                                    ACT.Gelu, bias=ff_b1[:, m + i:m + i + 1], scale=1.0 / W_SCALE)
                    last.then_inc(gelu_made, 1)
                    act.wait_ge(gelu_made, nth(it, len(HIDDENS), j))
                    nc.scalar.activation(h_T[0][:, to:to + 2, :].rearrange("p m n -> p (m n)"), gelu[:, j % 2],
                                         ACT.Copy).then_inc(hidden_high, 1)

            def body(b, items):
                slabs = iter(range(FIRST_SLABS, len(SLABS)))
                if isinstance(b, int) and b == 0:
                    act.wait_ge(vectors_loaded, 16 * VECTOR_LOADS)
                    act.wait_ge(w_split, len(SLABS))
                for kind, x in items:
                    it = b + offset(kind, x)
                    if not exists(it) and kind != "step":
                        continue
                    if kind == "bank":
                        empty_bank(b, it, BANK_USES.index(x))
                        if isinstance(b, int) and b == -1 and x[0] == "chunk" and (i := next(slabs, None)) is not None:
                            split(i)
                    elif kind == "high":
                        c = chunk_no(x)
                        act.wait_ge(roped_made, nth(it, len(QK), c))
                        act.wait_ge(bank_filled, turned(it, c - 2))
                        high = high_of(x[2], c)
                        src = roped[c % 2][:].rearrange("p (a two d) -> p a two d", two=2, d=DH)
                        if x[2] == "q":
                            src = src.unsqueeze(3).broadcast_to(list(high.shape)).rearrange("p a two c d -> p (a two) c d")
                            high = high.rearrange("p a two c d -> p (a two) c d")
                        else:
                            high = high[:, :, :, 0, :]
                        nc.scalar.activation(high, src, ACT.Copy).then_inc(roped_high, 1)
                    elif kind == "store":
                        act.wait_ge(residual_made, nth(it, len(RESIDUALS), RESIDUALS.index(("out", x, 1))))
                        act.dma_start(t["out"][bass.ds(it * SLOTS + x, 1), :, :].rearrange("b (t p) d -> p (b t) d", p=P),
                                      x_res[x][:]).then_inc(stored[x], 16)
                    elif kind == "step":
                        n, step = x
                        h = n * H + step
                        if exists(it):
                            act.wait_ge(max_made, nth(it, HEADS, h))
                            act.wait_ge(probs_turned, nth(it, HEADS, h - NP))
                            for tt in range(TT):
                                last = nc.scalar.activation(probs[h % NP][:, tt, :], ps_scores[h % 2][:, tt * N:(tt + 1) * N],
                                                            ACT.Exp, bias=neg_max[:, h % NP, tt:tt + 1],
                                                            accum_out=row_sum[:, h % NP, tt:tt + 1])
                            last.then_inc(probs_made, 1)
                        ith, h = back(it, n * H + step - PV_LAG - 1)
                        if exists(ith) and h % 4 == 3:
                            quad = h // 4
                            q = quad % 4
                            act.wait_ge(pv_made, nth(ith, HEADS, 4 * quad + 3))
                            if q == 0:
                                u = ("wo", (quad // 4 - 1) % len(PASSES), 1)
                                it_w = ith if quad else ith - 1
                                act.wait_ge(bank_filled, filled(it_w - offset("bank", u), BANK_USES.index(u)))
                            nc.scalar.activation(o_T[0][:, 2 * q:2 * q + 2, :].rearrange("p a n -> p (a n)"),
                                                 ps_o[quad % 2][:], ACT.Copy).then_inc(o_high_made, 1)

            body(-1, SCHEDULE)
            body(0, SCHEDULE)
            with act.Fori(1, ITERS - 1) as b:
                body(b, SCHEDULE)
            body(ITERS - 1, SCHEDULE)
            body(ITERS, SCHEDULE[:LAST_PART])
            for s in range(SLOTS):
                act.wait_ge(stored[s], CREDIT + 16 * ITERS)

        @block.tensor
        def _(pe):
            pe.wait_ge(ident_made, 3)
            pe.wait_ge(cond_loaded, 16 * 5)
            for k in range(KT):
                last = nc.tensor.transpose(bank[0][:, k * BATCH:(k + 1) * BATCH], cond[:, k * P:(k + 1) * P],
                                           ident[0:BATCH, 0:BATCH])
            last.then_inc(cond_turned, 1)
            pe.wait_ge(cond_copied, 1)
            for m, x in enumerate(("g1", "b1", "g2", "b2")):
                for dt in range(KT):
                    col = (m * KT + dt) * BATCH
                    for k in range(KT):
                        last = nc.tensor.matmul(bank[1][:, col:col + BATCH], w_cond[x][:, k, dt * P:(dt + 1) * P],
                                                cond_T[:, k, :], start=(k == 0), stop=(k == KT - 1))
            last.then_inc(cond_projected, 1)
            pe.wait_ge(cond_ready, 1)

            def product(dst, stationary, moving, first, last):
                terms = ((0, 0), (0, 1), (1, 0))
                for i, (a, b) in enumerate(terms):
                    mm = nc.tensor.matmul(dst, stationary[a], moving[b], start=first and i == 0,
                                          stop=last and i == len(terms) - 1)
                return mm

            def fill_bank(b, it, w):
                u = BANK_USES[w]
                dst = bank_of(w)
                if (before := emptied_for(b, w)) is not None:
                    pe.wait_ge(*before)
                if u[0] == "lnT":
                    pe.wait_ge(x_hat_made, normed(it, u[1]))
                    for k, (col, rows) in enumerate(widths(u[1][0])):
                        for tt in range(TT):
                            last = nc.tensor.transpose(dst[0:rows, k * N + tt * P:k * N + (tt + 1) * P],
                                                       x_hat[:, tt, col:col + rows], ident[:])
                elif u[0] == "chunk":
                    _, n, x, tt, half = u
                    kind = PASSES[n][0]
                    side = "ctx" if kind == "cross" and x != "q" else "ln"
                    weights = w_q[kind] if x == "q" else w_kv[kind]
                    col = half * CHUNK + (MID if x == "v" else 0)
                    if (x, tt, half) in (("q", 0, 0), ("k", 0, 0)):
                        if isinstance(b, int) and b <= 0:
                            pe.wait_ge(w_split, SPLIT[x, kind])
                        pe.wait_ge(a_T_ready, normed(it, (side, n)))
                    for k, (_, rows) in enumerate(widths(side)):
                        operand = [a[:, k, tt * P:(tt + 1) * P] for a in a_T[side]]
                        m = [w_part[:, k, col:col + CHUNK] for w_part in weights]
                        if rows == P:
                            last = product(dst[:], operand, m, k == 0, k == KT - 1)
                        else:
                            nc.tensor.matmul(dst[:], operand[0], m[0], start=False, stop=False)
                            last = nc.tensor.matmul(dst[:], operand[0][0:rows], m[1][0:rows], start=False, stop=True)
                elif u[0] == "turn":
                    _, n, x, tt, half = u
                    c = chunk_no(u)
                    pe.wait_ge(roped_low, nth(it, len(QK), c))
                    first, heads = (2 * CHUNK, CH_HEADS // 2) if x == "q_low" else (0, CH_HEADS)
                    for h in range(heads):
                        last = nc.tensor.transpose(dst[:].bitcast(F16)[:, h * P:(h + 1) * P],
                                                   roped_parts[c % 2][:, first + h * P:first + (h + 1) * P], ident_16[:])
                elif u[0] == "wo":
                    _, n, half = u
                    kind = PASSES[n][0]
                    pe.wait_ge(w_split, SPLIT["wo", kind])
                    pe.wait_ge(o_T_ready, nth(it, QUADS, 4 * n + 2 * half + 1))
                    tiles = range(half * MT // 2, (half + 1) * MT // 2)
                    for tt in range(TT):
                        for m in tiles:
                            last = product(dst[:, tt * D:(tt + 1) * D], [o[:, m, tt * P:(tt + 1) * P] for o in o_T],
                                           [a[:, m, :] for a in w_o[kind]], m == tiles[0], m == tiles[-1])
                elif u[0] == "hidden":
                    _, s, j = u
                    if j == 0:
                        pe.wait_ge(w_split, SPLIT["ff_w1"])
                        pe.wait_ge(a_T_ready, normed(it, ("ff", s)))
                    for i in range(2):
                        for k in range(KT):
                            last = product(dst[:, i * N:(i + 1) * N],
                                           [a[:, k, (2 * j + i) * P:(2 * j + i + 1) * P] for a in w_1],
                                           [a[:, k, :] for a in a_T["ff"]], k == 0, k == KT - 1)
                else:
                    _, s, half = u
                    pe.wait_ge(w_split, SPLIT["ff_w2"])
                    pe.wait_ge(hidden_ready, nth(it, len(HIDDENS), (2 * s + half + 1) * (len(HIDDENS) // 4) - 1))
                    for tt in range(TT):
                        for m in range(FF_HALF):
                            last = product(dst[:, tt * D:(tt + 1) * D], [a[:, m, tt * P:(tt + 1) * P] for a in h_T],
                                           [a[:, half * FF_HALF + m, :] for a in w_2], m == 0, m == FF_HALF - 1)
                return last

            def body(b, items):
                for kind, x in items:
                    it = b + offset(kind, x)
                    if kind == "bank":
                        w = BANK_USES.index(x)
                        if not exists(it):
                            stand_in(pe, bank_filled, filled(b, w))
                        else:
                            fill_bank(b, it, w).then_inc(bank_filled, 1)
                    elif kind == "step":
                        n, step = x
                        ith, h = back(it, n * H + step - TURN_LAG)
                        if exists(ith):
                            pe.wait_ge(probs_scaled, nth(ith, HEADS, h))
                            pe.wait_ge(probs_T_ready, nth(ith, HEADS, h - 1))
                            for tt in range(TT):
                                for m in range(TT):
                                    last = nc.tensor.transpose(
                                        ps_probs_T[:, m * N + tt * P:m * N + (tt + 1) * P],
                                        probs[h % NP][:, tt, m * P:(m + 1) * P], ident[:])
                            last.then_inc(probs_turned, 1)
                        h = n * H + step
                        if exists(it):
                            if step == 0:
                                count = nth(it, len(QK) // 2, (n + 1) * (len(QK) // 8) - 1)
                                pe.wait_ge(q_T_ready, count)
                                pe.wait_ge(q_low_T_ready, count)
                                pe.wait_ge(k_T_ready, count)
                            pe.wait_ge(probs_made, nth(it, HEADS, h - 2))
                            for tt in range(TT):
                                dst, keys = ps_scores[h % 2][:, tt * N:(tt + 1) * N], turned_parts["k"][n % 2]
                                nc.tensor.matmul(dst, turned_parts["q"][n % 2][:, step, tt * P:(tt + 1) * P],
                                                 keys[:, step, :], start=True, stop=False)
                                lo = DH * (step % 2)
                                last = nc.tensor.matmul(
                                    dst, turned_parts["q_low"][n % 2][lo:lo + DH, step // 2, tt * P:(tt + 1) * P],
                                    keys[lo:lo + DH, step, :], start=False, stop=True)
                            last.then_inc(scores_made, 1)
                    elif kind == "pv":
                        n, step = x
                        ith, h = back(it, n * H + step - PV_LAG)
                        if exists(ith):
                            n, head = divmod(h, H)
                            if head == 0:
                                pe.wait_ge(v_ready, nth(ith, len(V_CHUNKS), (n + 1) * (len(V_CHUNKS) // 4) - 1))
                            pe.wait_ge(probs_T_ready, nth(ith, HEADS, h))
                            quad = h // 4
                            if head % 4 == 0:
                                pe.wait_ge(o_T_ready, nth(ith, QUADS, quad - 2))
                            lo, col = DH * (head % 2), N * (head // 2 % 2)
                            for m in range(TT):
                                last = nc.tensor.matmul(ps_o[quad % 2][lo:lo + DH, col:col + N],
                                                        v[n % 2][:, m, head * DH:(head + 1) * DH],
                                                        probs_T[h % 2][:, m, :], start=(m == 0), stop=(m == TT - 1))
                            last.then_inc(pv_made, 1)

            body(-1, SCHEDULE)
            body(0, SCHEDULE)
            with pe.Fori(1, ITERS - 1) as b:
                body(b, SCHEDULE)
            body(ITERS - 1, SCHEDULE)
            body(ITERS, SCHEDULE[:LAST_PART])


INPUTS = ["x", "cond_1024", "ctx_768"] + [f"L0_xcond_{x}" for x in (
    "ln1_w", "ln1_b", "g1_w", "g1_b", "b1_w", "b1_b", "ln2_w", "ln2_b", "g2_w", "g2_b", "b2_w", "b2_b", "sa_wq",
    "sa_wkv", "sa_wo", "sa_bo", "ca_lnc_w", "ca_lnc_b", "ca_wq", "ca_wkv", "ca_wo", "ca_bo", "ff_w1", "ff_b1",
    "ff_w2", "ff_b2")]


def kernel(**inputs):
    import numpy as np
    import concourse.bacc as bacc
    from concourse.bass_utils import run_bass_kernel_spmd

    inv = (1.0 / 10000.0 ** (np.arange(0, DH, 2, dtype=np.float32) / DH)).astype(np.float32)
    angle = np.arange(N, dtype=np.float32)[:, None] * inv[None, :]
    cos = np.cos(angle)
    sin = np.stack((-np.sin(angle), np.sin(angle)), axis=-1).reshape(N, DH)
    scale = np.float32(DH ** -0.5)
    cos, sin = cos / np.float32(W_SCALE), sin / np.float32(W_SCALE)
    arrays = {"rope_cos_q": cos * scale, "rope_sin_q": sin * scale, "rope_cos_k": cos, "rope_sin_k": sin}
    arrays = {k: np.ascontiguousarray(a.astype(np.float32)) for k, a in arrays.items()}
    for name in INPUTS:
        arrays[name] = np.ascontiguousarray(inputs[name])

    nc = bacc.Bacc("TRN2", target_bir_lowering=False, num_devices=1)
    t = {k: nc.dram_tensor(f"in_{k}", a.shape, mybir.dt.from_np(a.dtype), kind="ExternalInput").ap()
         for k, a in arrays.items()}
    t["out"] = nc.dram_tensor("out_0", (BATCH, N, D), F32, kind="ExternalOutput").ap()
    block_kernel(nc, t)
    r = run_bass_kernel_spmd(nc, [{f"in_{k}": a for k, a in arrays.items()}], core_ids=[0])
    return r.results[0]["out_0"]
```
